# Optimizing a Trainium2 kernel written in Bass

```python
import numpy as np
import jax
import jax.numpy as jnp

def _softmax(x, axis=-1):
    return jax.nn.softmax(x, axis=axis)

def _gelu(x):
    return jax.nn.gelu(x, approximate=True)

def _silu(x):
    return jax.nn.silu(x)

def _sigmoid(x):
    return jax.nn.sigmoid(x)

def _layernorm(x, axis=-1, eps=1e-05):
    m = jnp.mean(x, axis=axis, keepdims=True)
    v = jnp.var(x, axis=axis, keepdims=True)
    return (x - m) / jnp.sqrt(v + eps)

def _scatter_add(tgt, idx, src, axis=0):
    return tgt.at[idx].add(src)

def _segment_sum(src, seg, n):
    return jax.ops.segment_sum(src, seg, n)
kernel_name = 'mk_seq_postln_d1_jaxref_r4_3f31a7'

def setup_inputs(seed: int=0):
    np.random.seed(seed)
    _w = jnp.asarray

    def _L0_attn_setup():
        import math
        import jax, jax.numpy as jnp
        import numpy as np
        NUM_HEADS = 32
        HIDDEN = 1024
        HEAD_DIM = HIDDEN // NUM_HEADS
        NEG_INF = -1e+30

        def _alibi_slopes(n: int) -> jnp.ndarray:
            cp2 = 2 ** math.floor(math.log2(n))
            base = 2.0 ** (-2.0 ** (-(math.log2(cp2) - 3)))
            slopes = base ** np.arange(1, cp2 + 1, dtype=np.float64)
            if cp2 != n:
                extra_base = 2.0 ** (-2.0 ** (-(math.log2(2 * cp2) - 3)))
                rem = min(cp2, n - cp2)
                extra = extra_base ** np.arange(1, 1 + 2 * rem, 2, dtype=np.float64)
                slopes = np.concatenate([slopes, extra])
            return jnp.asarray(slopes, dtype=jnp.float32)
        key = jax.random.key(seed)
        k1, k2, k3 = jax.random.split(key, 3)
        B, S = (2, 512)
        hidden_states = jax.random.normal(k1, (B, S, HIDDEN), dtype=jnp.float32)
        Wqkv = jax.random.normal(k2, (HIDDEN, NUM_HEADS * HEAD_DIM + 2 * HEAD_DIM), dtype=jnp.float32) * 0.02
        Wo = jax.random.normal(k3, (HIDDEN, HIDDEN), dtype=jnp.float32) * 0.02
        return {'hidden_states': hidden_states, 'Wqkv': Wqkv, 'Wo': Wo}
    _L0_attn_in = _L0_attn_setup()

    def _L0_ffn_setup():
        import jax, jax.numpy as jnp
        import numpy as np
        GROUP_SIZE = 128
        QMAX = 7.0
        QMIN = -8.0

        def quantize_dequantize(w):
            out_f, in_f = w.shape
            wg = w.reshape(out_f, in_f // GROUP_SIZE, GROUP_SIZE)
            absmax = jnp.max(jnp.abs(wg), axis=-1, keepdims=True)
            scale = absmax / QMAX
            safe_scale = jnp.where(scale > 0, scale, 1.0)
            q = jnp.clip(jnp.round(wg / safe_scale), QMIN, QMAX)
            wq = q * scale
            return wq.reshape(out_f, in_f)
        key = jax.random.key(seed)
        k1, k2, k3 = jax.random.split(key, 3)
        B, S, D_IN, D_OUT = (4, 512, 1024, 1024)
        x = jax.random.normal(k1, (B, S, D_IN), dtype=jnp.float32)
        weight = jax.random.normal(k2, (D_OUT, D_IN), dtype=jnp.float32) * 0.02
        bias = jax.random.normal(k3, (D_OUT,), dtype=jnp.float32) * 0.02
        return {'x': x, 'weight': weight, 'bias': bias}
    _L0_ffn_in = _L0_ffn_setup()
    _d = {'L0_attn_hidden_states': _L0_attn_in['hidden_states'], 'L0_attn_Wqkv': _L0_attn_in['Wqkv'], 'L0_attn_Wo': _L0_attn_in['Wo'], 'L0_ffn_weight': _L0_ffn_in['weight'], 'L0_ffn_bias': _L0_ffn_in['bias']}
    _x0 = _d['L0_attn_hidden_states']
    _d['L0_attn_hidden_states'] = jax.random.normal(jax.random.fold_in(jax.random.key(seed), 1), (4, 1024, 1024), dtype=_x0.dtype)
    del _x0
    return _d

def reference(L0_attn_hidden_states, L0_attn_Wqkv, L0_attn_Wo, L0_ffn_weight, L0_ffn_bias):

    def _L0_attn_ref(hidden_states, Wqkv, Wo):
        import math
        import jax, jax.numpy as jnp
        import numpy as np
        NUM_HEADS = 32
        HIDDEN = 1024
        HEAD_DIM = HIDDEN // NUM_HEADS
        NEG_INF = -1e+30

        def _alibi_slopes(n: int) -> jnp.ndarray:
            cp2 = 2 ** math.floor(math.log2(n))
            base = 2.0 ** (-2.0 ** (-(math.log2(cp2) - 3)))
            slopes = base ** np.arange(1, cp2 + 1, dtype=np.float64)
            if cp2 != n:
                extra_base = 2.0 ** (-2.0 ** (-(math.log2(2 * cp2) - 3)))
                rem = min(cp2, n - cp2)
                extra = extra_base ** np.arange(1, 1 + 2 * rem, 2, dtype=np.float64)
                slopes = np.concatenate([slopes, extra])
            return jnp.asarray(slopes, dtype=jnp.float32)
        B, S, H = hidden_states.shape
        nH, d = (NUM_HEADS, HEAD_DIM)
        scale = d ** (-0.5)
        qkv = hidden_states @ Wqkv
        q = qkv[..., :nH * d].reshape(B, S, nH, d)
        k = qkv[..., nH * d:nH * d + d]
        v = qkv[..., nH * d + d:]
        scores = jnp.einsum('bqhd,bkd->bhqk', q, k) * scale
        pos_q = jnp.arange(S)[:, None]
        pos_k = jnp.arange(S)[None, :]
        slopes = _alibi_slopes(nH)
        alibi = slopes[:, None, None] * (pos_k - pos_q).astype(jnp.float32)
        causal = pos_k <= pos_q
        scores = jnp.where(causal[None, None], scores + alibi[None], NEG_INF)
        probs = jax.nn.softmax(scores, axis=-1)
        attn = jnp.einsum('bhqk,bkd->bqhd', probs, v).reshape(B, S, H)
        return attn @ Wo

    def _L0_ffn_ref(x, weight, bias):
        import jax, jax.numpy as jnp
        import numpy as np
        GROUP_SIZE = 128
        QMAX = 7.0
        QMIN = -8.0

        def quantize_dequantize(w):
            out_f, in_f = w.shape
            wg = w.reshape(out_f, in_f // GROUP_SIZE, GROUP_SIZE)
            absmax = jnp.max(jnp.abs(wg), axis=-1, keepdims=True)
            scale = absmax / QMAX
            safe_scale = jnp.where(scale > 0, scale, 1.0)
            q = jnp.clip(jnp.round(wg / safe_scale), QMIN, QMAX)
            wq = q * scale
            return wq.reshape(out_f, in_f)
        w_q = quantize_dequantize(weight)
        w = weight + jax.lax.stop_gradient(w_q - weight)
        return jnp.einsum('bsd,od->bso', x, w) + bias
    x = L0_attn_hidden_states
    x = _layernorm(x + _L0_attn_ref(x, L0_attn_Wqkv, L0_attn_Wo), axis=-1)
    x = _layernorm(x + _L0_ffn_ref(x, L0_ffn_weight, L0_ffn_bias), axis=-1)
    return x

_drawn_inputs = setup_inputs


def setup_inputs(seed=0):
    import zlib

    import numpy as np

    out = dict(_drawn_inputs(seed))
    spreads = {}
    factors = {'L0_ffn_bias': 3.407}
    for name, (base, spread) in spreads.items():
        noise = np.random.default_rng([zlib.crc32(name.encode()), seed]).standard_normal(out[name].shape)
        drawn = base * np.exp(spread * noise) if base else spread * noise
        out[name] = jnp.asarray(drawn.astype(out[name].dtype))
    for name, factor in factors.items():
        out[name] = (out[name] * factor).astype(out[name].dtype)
    return out
```

```python
import concourse.bass as bass
from concourse import mybir
from contextlib import ExitStack
import numpy as np

P = 128
B, S, H = 4, 1024, 1024
NH, D = 32, 32
T = B * S
KT = H // P
HPG = P // D
NG = NH // HPG
CH = 512
NCH = T // CH
QKV = NH * D + 2 * D
EPS = 1e-5
QMAX, QMIN = 7.0, -8.0
ROUND = 1.5 * 2.0 ** 23
MASKED = -1e30
SPANS = 16
CREDIT = 16

fp32 = mybir.dt.float32
f32r = mybir.dt.float32r
bf16 = mybir.dt.bfloat16
ALU = mybir.AluOpType
ACT = mybir.ActivationFunctionType
AXX = mybir.AxisListType.X


def slopes():
    base = 2.0 ** (-2.0 ** (-(np.log2(NH) - 3)))
    return (base ** np.arange(1, NH + 1, dtype=np.float64)).astype(np.float32)


def shape_constants():
    sl = slopes()
    head = np.arange(NG)[None, :] * HPG + np.arange(P)[:, None] // D
    qscale = (np.float64(D) ** -0.5 / sl.astype(np.float64)[head]).astype(np.float32)
    rel = np.arange(S)[None, :] - (S - P) - np.arange(P)[:, None]
    distance = np.where(rel <= 0, rel, MASKED).astype(np.float32)
    pos, starts = np.arange(S), np.arange(SPANS)[:, None] * (S // SPANS)
    q_rows = np.concatenate([[np.ones(S), -pos, np.zeros(S), np.zeros(S)], np.where(pos < starts, MASKED, 0.0)])
    k_rows = np.concatenate([[pos, np.ones(S), np.ones(S), np.ones(S)], (pos >= starts) & (pos < starts + S // SPANS)])
    q_rows, k_rows = q_rows.astype(np.float32), k_rows.astype(np.float32)
    slope = np.broadcast_to(sl[None, :], (P, NH)).astype(np.float32)
    return {"c_qscale": qscale, "c_distance": distance, "c_qrows": q_rows, "c_krows": k_rows,
            "c_ident": np.eye(P, dtype=np.float32), "c_slope": np.ascontiguousarray(slope)}


class Tally:
    def __init__(self, eng, name, first):
        self.eng, self.reg = eng, eng.alloc_register(name)
        eng.reg_mov(self.reg, first)

    def wait(self, sem, value, to_next):
        if isinstance(value, int):
            self.eng.wait_ge(sem, value)
        else:
            self.eng.wait_ge(sem, self.reg)
            self.eng.reg_add(self.reg, self.reg, to_next)


def raw(ap):
    return ap.bitcast(fp32)


def run_loop(eng, total, unroll, body):
    trips = (total - 1) // unroll
    with eng.Fori(0, trips) as i:
        for u in range(unroll):
            body(i * unroll + u, u, i)
    for t in range(trips * unroll, total):
        body(t, t % unroll, t // unroll)


def edge_loop(eng, total, body):
    for t in range(2):
        body(t, t, 0)
    with eng.Fori(1, total // 2 - 1) as i:
        for u in range(2):
            body(i * 2 + u, u, i)
    for t in range(total - 2, total):
        body(t, t % 2, t // 2)


class Ring:
    def __init__(self, K, banks):
        self.K = K
        self.bank = [n % banks for n in range(K)]
        self.prev = []
        for n in range(K):
            before = [m for m in range(n) if self.bank[m] == self.bank[n]]
            last = [m - K for m in range(K) if self.bank[m] == self.bank[n]]
            self.prev.append(before[-1] if before else last[-1])

    def free(self, t, n):
        return t * self.K + (self.K + self.prev[n] + 1)


def layer(nc, x, wqkv, wo, wf, bias, qscale, distance, qrows, krows, ident_h, slope_h, out):
    def dram(name, shape, dt):
        return nc.dram_tensor(name, shape, dt, kind="Internal").ap()

    q_hi_d = dram("q_hi_d", [NG, P, T], fp32)
    q_lo_d = dram("q_lo_d", [NG, P, T], fp32)
    k_d = dram("k_d", [3 * D, T], fp32)
    v_d = dram("v_d", [P, T // P, D], fp32)
    att_d = dram("att_d", [NG, P, T], fp32)
    wo_d = dram("wo_d", [2, P, KT, H], fp32)
    wf_d = dram("wf_d", [2, P, KT, H], fp32)
    project(nc, x, wqkv, wo, wf, qscale, ident_h, q_hi_d, q_lo_d, k_d, v_d, wo_d, wf_d)
    attend(nc, distance, qrows, krows, ident_h, slope_h, q_hi_d, q_lo_d, k_d, v_d, att_d)
    finish(nc, x, bias, ident_h, att_d, wo_d, wf_d, out)


def project(nc, x, wqkv, wo, wf, qscale_h, ident_h, q_hi_d, q_lo_d, k_d, v_d, wo_d, wf_d):
    x_v = x.rearrange("b s h -> (b s) h").rearrange("(c s p) h -> p c s h", p=P, s=CH // P)
    SUB = CH // P
    QC = NG
    MM = QC + 1
    TR = KT + 2 + 1
    mm_ring, tr_ring = Ring(MM, 4), Ring(TR, 4)
    TR_V, TR_X, TR_W = 0, 1, 1 + KT
    SCALE_STEPS, QUOT_STEPS = 12, 12
    QSTEPS = SCALE_STEPS + 2 * QUOT_STEPS + 5

    ctx = ExitStack()
    with ctx:
        def sb(name, shape, dt=fp32):
            return ctx.enter_context(nc.sbuf_tensor(name, shape, dt))

        def sem(name):
            return ctx.enter_context(nc.semaphore(name))

        wq_hi, wq_lo = sb("wq_hi", [P, KT, QKV], f32r), sb("wq_lo", [P, KT, QKV], f32r)
        x_in = sb("x_in", [P, SUB, H])
        xt_hi, xt_lo = sb("xt_hi", [P, 2, KT, CH], f32r), sb("xt_lo", [P, 2, KT, CH], f32r)
        stage = sb("stage", [P, 4, QKV])
        q_hi, q_lo = sb("q_hi", [P, 2, CH], f32r), sb("q_lo", [P, 2, CH], f32r)
        k_hi, k_lo = sb("k_hi", [D, CH], f32r), sb("k_lo", [D, CH], f32r)
        vt = sb("vt", [D, CH])
        v_sb = sb("v_sb", [P, SUB, D])
        wf_hi, wf_lo = sb("wf_hi", [P, KT, P], f32r), sb("wf_lo", [P, KT, P], f32r)
        wo_hi, wo_lo = sb("wo_hi", [P, H], f32r), sb("wo_lo", [P, H], f32r)
        ident = sb("ident1", [P, P])
        qscale = sb("qscale", [P, NG])
        seven, credit = sb("seven", [P, KT]), sb("credit", [P, 6])
        top, low, absmax, scale, isz, safe, scale0, rest, inv, half_lo = (sb(f"quant{n}", [P, KT]) for n in range(10))
        half_hi = sb("half_hi", [P, KT], f32r)
        quot_hi, quot_lo, part = sb("quot_hi", [P, KT // 2, P], f32r), sb("quot_lo", [P, KT // 2, P]), sb("part", [P, KT // 2, P])
        psum = [ctx.enter_context(nc.psum_tensor(f"ps{n}", [P, CH], fp32)) for n in range(8)]
        mm_ps, tr_ps = psum[:4], psum[4:]

        consts_in = sem("consts_in")
        wq_in = [sem(f"wq_in{n}") for n in range(4)]
        wq_hi_done, wq_lo_done = sem("wq_hi_done"), sem("wq_lo_done")
        x_loaded = sem("x_loaded")
        tr_done, tr_hi, tr_free = sem("tr_done"), sem("tr_hi"), sem("tr_free")
        mm_done, mm_hi, mm_free = sem("mm_done"), sem("mm_hi"), sem("mm_free")
        q_stored = [sem(f"q_stored{n}") for n in range(2)]
        kv_stored, vt_ready = sem("kv_stored"), sem("vt_ready")
        w_loaded, wo_loaded = sem("w_loaded"), sem("wo_loaded")
        quant_steps = sem("quant_steps")
        wo_hi_done, wo_lo_done = sem("wo_hi_done"), sem("wo_lo_done")
        wf_stored, wo_stored = sem("wf_stored"), sem("wo_stored")
        block = ctx.enter_context(nc.Block())

        w_blk = wf.rearrange("(t p) i -> p t i", p=P)
        wo_blk = wo.rearrange("(t p) o -> p t o", p=P)
        W_STAGE, WO_STAGE = 0, 3

        def tr_uses(t, n):
            skipped = KT if isinstance(t, int) and t == NCH - 1 and n >= TR_W else 0
            return t * TR + (KT + n + 1 - skipped)

        def tr_freed(t, n):
            return tr_uses(t, n) + TR

        @block.sync
        def _(sp):
            sp.dma_start(ident[:, :], ident_h).then_inc(consts_in, 16)
            sp.dma_start(qscale[:, :], qscale_h).then_inc(consts_in, 16)
            sp.dma_start(x_in[:, :, :], x_v[:, 0, :, :]).then_inc(x_loaded, 16)
            for k in range(KT):
                if k >= 4:
                    sp.wait_ge(wq_hi_done, k - 3)
                    sp.wait_ge(wq_lo_done, k - 3)
                sp.dma_start(stage[:, k % 4, :], wqkv[k * P:(k + 1) * P, :]).then_inc(wq_in[k % 4], 16)
            sp.wait_ge(tr_done, KT)
            sp.dma_start(x_in[:, :, :], x_v[:, 1, :, :]).then_inc(x_loaded, 16)
            sp.wait_ge(wq_hi_done, KT)
            sp.wait_ge(wq_lo_done, KT)
            sp.dma_start(stage[:, W_STAGE, 0:H], w_blk[:, 0, :]).then_inc(w_loaded, 16)
            sp.dma_start(stage[:, WO_STAGE, 0:H], wo_blk[:, 0, :]).then_inc(wo_loaded, 16)

            def body(t, u, i):
                last, before_last = isinstance(t, int) and t == NCH - 1, isinstance(t, int) and t == NCH - 2
                tok = bass.ds(t * CH, CH)
                sp.wait_ge(mm_free, t * MM + MM + 1)
                for row, half in ((0, k_hi), (D, k_lo), (2 * D, k_hi)):
                    sp.dma_start(k_d[row:row + D, tok], raw(half[:, :])).then_inc(kv_stored, 16)
                sp.wait_ge(wo_lo_done, t + 1)
                for n, half in enumerate((wo_hi, wo_lo)):
                    sp.dma_start(wo_d[n, :, bass.ds(t, 1), :], raw(half[:, :])[:, None, :]).then_inc(wo_stored, 16)
                if not last:
                    sp.dma_start(stage[:, WO_STAGE:WO_STAGE + 1, 0:H], wo_blk[:, bass.ds(t + 1, 1), :]).then_inc(wo_loaded, 16)
                for c in range(QC):
                    sp.wait_ge(mm_free, t * MM + MM + 2 + c)
                    sp.dma_start(q_hi_d[c, :, tok], raw(q_hi[:, c % 2, :])).then_inc(q_stored[c % 2], 16)
                    sp.dma_start(q_lo_d[c, :, tok], raw(q_lo[:, c % 2, :])).then_inc(q_stored[c % 2], 16)
                    if c == 1:
                        sp.wait_ge(tr_free, tr_freed(t, TR_V))
                        sp.dma_start(v_d[:, bass.ds(t * SUB, SUB), :], v_sb[:, :, :]).then_inc(kv_stored, 16)
                    if c == 5 and not last and not before_last:
                        sp.wait_ge(tr_done, tr_uses(t, TR_X + KT - 1))
                        sp.dma_start(x_in[:, None, :, :], x_v[:, bass.ds(t + 2, 1), :, :]).then_inc(x_loaded, 16)
                sp.wait_ge(tr_free, tr_freed(t, TR_W + 1))
                for n, half in enumerate((wf_hi, wf_lo)):
                    sp.dma_start(wf_d[n, :, :, bass.ds(t * P, P)], raw(half[:, :, :])).then_inc(wf_stored, 16)
                if not last:
                    sp.dma_start(stage[:, W_STAGE:W_STAGE + 1, 0:H], w_blk[:, bass.ds(t + 1, 1), :]).then_inc(w_loaded, 16)

            run_loop(sp, NCH, 2, body)
            for n in range(2):
                sp.wait_ge(q_stored[n], NCH * QC // 2 * 32 + CREDIT)
            sp.wait_ge(kv_stored, NCH * 64 + CREDIT)
            sp.wait_ge(wo_stored, NCH * 32 + CREDIT)
            sp.wait_ge(wf_stored, NCH * 32 + CREDIT)

        @block.gpsimd
        def _(pool):
            pool.memset(seven[:, :], QMAX).then_inc(tr_free, TR)
            pool.memset(credit[:, 0:1], 0.0).then_inc(mm_free, MM)
            for n, stored in enumerate((kv_stored, wo_stored, wf_stored, q_stored[0], q_stored[1])):
                pool.memset(credit[:, n + 1:n + 2], 0.0).then_inc(stored, CREDIT)

        @block.tensor
        def _(pe):
            def product(t, u, c):
                pe.wait_ge(mm_free, mm_ring.free(t, c))
                cols = slice(NH * D, QKV) if c == 0 else slice((c - 1) * P, c * P)
                o = mm_ps[mm_ring.bank[c]][0:cols.stop - cols.start, :]
                for k in range(KT):
                    for n, (w, xt) in enumerate(((wq_hi, xt_hi), (wq_hi, xt_lo), (wq_lo, xt_hi))):
                        last = nc.tensor.matmul(o, w[:, k, cols], xt[:, u, k, :], start=(k == 0 and n == 0),
                                                stop=(k == KT - 1 and n == 2))
                last.then_inc(mm_done, 1)

            def transpose_x(bank, k):
                for s in range(SUB):
                    last = nc.tensor.transpose(bank[:, s * P:(s + 1) * P], x_in[:, s, k * P:(k + 1) * P], ident[:, :])
                last.then_inc(tr_done, 1)

            v_chunks = Tally(pe, "v_chunks", 1)
            pe.wait_ge(consts_in, 32)
            pe.wait_ge(x_loaded, 16)
            for k in range(KT):
                if k >= 4:
                    pe.wait_ge(tr_free, TR + k - 3)
                transpose_x(tr_ps[k % 4], k)
            pe.wait_ge(wq_lo_done, KT)
            pe.wait_ge(tr_free, TR + KT)

            def body(t, u, i):
                last = isinstance(t, int) and t == NCH - 1
                pe.wait_ge(tr_free, t * TR + (KT + TR_X + KT))
                for c in range(MM):
                    product(t, u, c)
                    if c == 1:
                        pe.wait_ge(tr_free, KT + tr_ring.free(t, TR_V))
                        v_chunks.wait(vt_ready, t + 1, 1)
                        bank = tr_ps[tr_ring.bank[TR_V]]
                        for s in range(SUB):
                            done = nc.tensor.transpose(bank[:, s * D:(s + 1) * D], vt[:, s * P:(s + 1) * P], ident[0:D, 0:D])
                        done.then_inc(tr_done, 1)
                    if c == 3 and not last:
                        pe.wait_ge(x_loaded, t * 16 + 32)
                    if 3 <= c <= 6 and not last:
                        for k in (2 * (c - 3), 2 * (c - 3) + 1):
                            pe.wait_ge(tr_free, KT + tr_ring.free(t, TR_X + k))
                            transpose_x(tr_ps[tr_ring.bank[TR_X + k]], k)
                    if c == 7:
                        pe.wait_ge(quant_steps, t * QSTEPS + QSTEPS)
                        for h in range(2):
                            pe.wait_ge(tr_free, tr_freed(t, TR_W + h) - 1 - h if last else KT + tr_ring.free(t, TR_W + h))
                            bank = tr_ps[tr_ring.bank[TR_W + h]]
                            for j in range(4):
                                i = h * 4 + j
                                done = nc.tensor.transpose(bank[:, j * P:(j + 1) * P], stage[:, 2, i * P:(i + 1) * P], ident[:, :])
                            done.then_inc(tr_done, 1)

            run_loop(pe, NCH, 2, body)

        @block.scalar
        def _(act):
            act.wait_ge(consts_in, 32)
            for k in range(KT):
                act.wait_ge(tr_done, k + 1)
                nc.scalar.copy(xt_hi[:, 0, k, :], tr_ps[k % 4][:, :]).then_inc(tr_hi, 1)
            for k in range(KT):
                act.wait_ge(wq_in[k % 4], 16 * (k // 4 + 1))
                nc.scalar.copy(wq_hi[:, k, :], stage[:, k % 4, :]).then_inc(wq_hi_done, 1)

            def body(t, u, i):
                last = isinstance(t, int) and t == NCH - 1
                act.wait_ge(wo_loaded, t * 16 + 16)
                act.wait_ge(wo_stored, t * 32 + CREDIT)
                nc.scalar.copy(wo_hi[:, :], stage[:, WO_STAGE, 0:H]).then_inc(wo_hi_done, 1)
                for c in range(MM):
                    act.wait_ge(mm_done, t * MM + c + 1)
                    bank = mm_ps[mm_ring.bank[c]]
                    if c == 0:
                        act.wait_ge(kv_stored, t * 64 + CREDIT)
                        nc.scalar.copy(vt[:, :], bank[D:2 * D, :]).then_inc(vt_ready, 1)
                        nc.scalar.copy(k_hi[:, :], bank[0:D, :]).then_inc(mm_hi, 1)
                    else:
                        act.wait_ge(q_stored[(c - 1) % 2], t * (32 * QC // 2) + 32 * ((c - 1) // 2) + CREDIT)
                        nc.scalar.activation(q_hi[:, (c - 1) % 2, :], bank[:, :], ACT.Copy,
                                             scale=qscale[:, c - 1:c]).then_inc(mm_hi, 1)
                    if 3 <= c <= 6 and not last:
                        for k in (2 * (c - 3), 2 * (c - 3) + 1):
                            act.wait_ge(tr_done, tr_uses(t, TR_X + k))
                            nc.scalar.copy(xt_hi[:, 1 - u, k, :], tr_ps[tr_ring.bank[TR_X + k]][:, :]).then_inc(tr_hi, 1)
                    if c == 7:
                        act.wait_ge(wf_stored, t * 32 + CREDIT)
                        for h in range(2):
                            act.wait_ge(tr_done, tr_uses(t, TR_W + h))
                            nc.scalar.copy(wf_hi[:, h * 4:h * 4 + 4, :], tr_ps[tr_ring.bank[TR_W + h]][:, :]
                                           .rearrange("p (j o) -> p j o", o=P)).then_inc(tr_hi, 1)

            run_loop(act, NCH, 2, body)

        @block.vector
        def _(dve):
            for k in range(KT):
                dve.wait_ge(tr_hi, k + 1)
                nc.vector.tensor_tensor(xt_lo[:, 0, k, :], tr_ps[k % 4][:, :], raw(xt_hi[:, 0, k, :]),
                                        ALU.subtract).then_inc(tr_free, 1)
            for k in range(KT):
                dve.wait_ge(wq_hi_done, k + 1)
                nc.vector.tensor_tensor(wq_lo[:, k, :], stage[:, k % 4, :], raw(wq_hi[:, k, :]),
                                        ALU.subtract).then_inc(wq_lo_done, 1)

            w = stage[:, W_STAGE, 0:H].rearrange("p (g i) -> p g i", i=P)
            q = stage[:, 1, 0:H].rearrange("p (g i) -> p g i", i=P)
            r = stage[:, 2, 0:H].rearrange("p (g i) -> p g i", i=P)

            def quantizer(t, done):
                steps = [done]

                def step(ins):
                    steps[0] += 1
                    ins.then_inc(quant_steps, 1)
                    if steps[0] < QSTEPS:
                        dve.wait_ge(quant_steps, t * QSTEPS + steps[0])
                return step, steps

            def group_scales(t):
                step, steps = quantizer(t, 0)
                dve.wait_ge(w_loaded, t * 16 + 16)
                nc.vector.tensor_reduce(top[:, :], w, AXX, ALU.max)
                step(nc.vector.tensor_reduce(low[:, :], w, AXX, ALU.min))
                step(nc.vector.scalar_tensor_tensor(out=absmax[:, :], in0=low[:, :], scalar=-1.0, in1=top[:, :],
                                                    op0=ALU.mult, op1=ALU.max))
                step(nc.vector.tensor_scalar(scale0[:, :], absmax[:, :], 1.0 / QMAX, None, ALU.mult))
                step(nc.vector.tensor_copy(half_hi[:, :], scale0[:, :]))
                step(nc.vector.tensor_tensor(half_lo[:, :], scale0[:, :], raw(half_hi[:, :]), ALU.subtract))
                step(nc.vector.scalar_tensor_tensor(out=rest[:, :], in0=raw(half_hi[:, :]), scalar=-QMAX, in1=absmax[:, :],
                                                    op0=ALU.mult, op1=ALU.add))
                step(nc.vector.scalar_tensor_tensor(out=rest[:, :], in0=half_lo[:, :], scalar=-QMAX, in1=rest[:, :],
                                                    op0=ALU.mult, op1=ALU.add))
                step(nc.vector.scalar_tensor_tensor(out=scale[:, :], in0=rest[:, :], scalar=1.0 / QMAX, in1=scale0[:, :],
                                                    op0=ALU.mult, op1=ALU.add))
                step(nc.vector.tensor_scalar(isz[:, :], scale[:, :], 0.0, None, ALU.is_le))
                step(nc.vector.tensor_tensor(safe[:, :], scale[:, :], isz[:, :], ALU.add))
                nc.vector.reciprocal(inv[:, :], safe[:, :])
                step(nc.vector.tensor_copy(half_hi[:, :], safe[:, :]))
                step(nc.vector.tensor_tensor(half_lo[:, :], safe[:, :], raw(half_hi[:, :]), ALU.subtract))
                assert steps[0] == SCALE_STEPS

            def quotients(t, n):
                step, steps = quantizer(t, SCALE_STEPS + n * QUOT_STEPS)
                g = slice(n * KT // 2, (n + 1) * KT // 2)
                bc = lambda a: a[:, g, None].to_broadcast([P, KT // 2, P])
                tt = nc.vector.tensor_tensor
                if n == 0:
                    dve.wait_ge(tr_done, t * TR + KT)
                step(tt(q[:, g, :], w[:, g, :], bc(inv), ALU.mult))
                step(nc.vector.tensor_copy(quot_hi[:, :, :], q[:, g, :]))
                tt(quot_lo[:, :, :], q[:, g, :], raw(quot_hi[:, :, :]), ALU.subtract)
                step(tt(part[:, :, :], raw(quot_hi[:, :, :]), bc(raw(half_hi[:, :])), ALU.mult))
                step(tt(r[:, g, :], w[:, g, :], part[:, :, :], ALU.subtract))
                for a, b in ((raw(quot_hi[:, :, :]), half_lo), (quot_lo[:, :, :], raw(half_hi[:, :])), (quot_lo[:, :, :], half_lo)):
                    step(tt(part[:, :, :], a, bc(b), ALU.mult))
                    step(tt(r[:, g, :], r[:, g, :], part[:, :, :], ALU.subtract))
                step(tt(r[:, g, :], r[:, g, :], bc(inv), ALU.mult))
                step(tt(q[:, g, :], q[:, g, :], r[:, g, :], ALU.add))
                assert steps[0] == SCALE_STEPS + (n + 1) * QUOT_STEPS

            def fake_quantized(t):
                step, steps = quantizer(t, SCALE_STEPS + 2 * QUOT_STEPS)
                bc = scale[:, :, None].to_broadcast([P, KT, P])
                step(nc.vector.tensor_scalar(q, q, ROUND, ROUND, ALU.add, ALU.subtract))
                step(nc.vector.tensor_scalar(q, q, QMAX, QMIN, ALU.min, ALU.max))
                step(nc.vector.tensor_tensor(q, q, bc, ALU.mult))
                step(nc.vector.tensor_tensor(q, q, w, ALU.subtract))
                step(nc.vector.tensor_tensor(r, w, q, ALU.add))
                assert steps[0] == QSTEPS

            def body(t, u, i):
                last = isinstance(t, int) and t == NCH - 1
                dve.wait_ge(wo_hi_done, t + 1)
                dve.wait_ge(wo_stored, t * 32 + CREDIT)
                nc.vector.tensor_tensor(wo_lo[:, :], stage[:, WO_STAGE, 0:H], raw(wo_hi[:, :]),
                                        ALU.subtract).then_inc(wo_lo_done, 1)
                for c in range(MM):
                    dve.wait_ge(mm_hi, t * MM + c + 1)
                    bank = mm_ps[mm_ring.bank[c]]
                    if c == 0:
                        dve.wait_ge(kv_stored, t * 64 + CREDIT)
                        nc.vector.tensor_tensor(k_lo[:, :], bank[0:D, :], raw(k_hi[:, :]), ALU.subtract).then_inc(mm_free, 1)
                    else:
                        dve.wait_ge(q_stored[(c - 1) % 2], t * (32 * QC // 2) + 32 * ((c - 1) // 2) + CREDIT)
                        nc.vector.scalar_tensor_tensor(out=q_lo[:, (c - 1) % 2, :], in0=bank[:, :], scalar=qscale[:, c - 1:c],
                                                       in1=raw(q_hi[:, (c - 1) % 2, :]),
                                                       op0=ALU.mult, op1=ALU.subtract).then_inc(mm_free, 1)
                    if c == 0:
                        group_scales(t)
                    elif c <= 2:
                        quotients(t, c - 1)
                    elif c == 3:
                        fake_quantized(t)
                    if c == 1:
                        dve.wait_ge(tr_done, tr_uses(t, TR_V))
                        nc.vector.tensor_copy(v_sb[:, :, :], tr_ps[tr_ring.bank[TR_V]][:, 0:SUB * D]
                                              .rearrange("p (s d) -> p s d", d=D)).then_inc(tr_free, 1)
                    if 3 <= c <= 6 and not last:
                        for k in (2 * (c - 3), 2 * (c - 3) + 1):
                            dve.wait_ge(tr_hi, t * (KT + 2) + (KT + k + 1))
                            nc.vector.tensor_tensor(xt_lo[:, 1 - u, k, :], tr_ps[tr_ring.bank[TR_X + k]][:, :],
                                                    raw(xt_hi[:, 1 - u, k, :]), ALU.subtract).then_inc(tr_free, 1)
                    if c == 7:
                        dve.wait_ge(wf_stored, t * 32 + CREDIT)
                        for h in range(2):
                            dve.wait_ge(tr_hi, t * (KT + 2) + (KT + h + 1 + (0 if last else KT)))
                            nc.vector.tensor_tensor(wf_lo[:, h * 4:h * 4 + 4, :],
                                                    tr_ps[tr_ring.bank[TR_W + h]][:, :].rearrange("p (j o) -> p j o", o=P),
                                                    raw(wf_hi[:, h * 4:h * 4 + 4, :]), ALU.subtract).then_inc(tr_free, 1)

            run_loop(dve, NCH, 2, body)


def attend(nc, distance_h, qrows_h, krows_h, ident_h, slope_h, q_hi_d, q_lo_d, k_d, v_d, att_d):
    ITS = B * NG
    QB = S // P
    HALF = S // CH
    BPH = CH // P
    KR = 3 * D + 4 + SPANS
    SLOTS = 3

    pieces = [(0, h, qb, 0, (qb + 1) * P) for h in range(HPG) for qb in range(BPH)]
    pieces += [(1, h, qb, k0, min((qb + 1) * P - k0, CH)) for h in range(HPG) for qb in range(BPH, QB) for k0 in (0, CH)]
    units = [(c, i) for c in range(HALF) for i in range(BPH * (c + 1))]

    def span(unit):
        c, i = unit
        lo = max(CH * c, P * i)
        return lo, CH * (c + 1) - lo

    def heads_at_once(unit):
        return {CH: 1, 3 * P: 1, 2 * P: 2, P: 4}[span(unit)[1]]

    scores_of, n = [], 0
    for unit in units:
        scores_of.append(n)
        n += HPG // heads_at_once(unit)
    SC = n
    NU = len(units)
    share = [4, 4, 3, 3, 5, 5, 5, 5, 5, 4, 2, 3]
    assert sum(share) == len(pieces)
    T_AT = {6: 0, 11: 1}
    MX = len(pieces) + len(T_AT)
    EXPS = HPG * NU
    exps_through = []
    for n, unit in enumerate(units):
        exps_through += [HPG * n + heads_at_once(unit) * (j + 1) for j in range(HPG // heads_at_once(unit))]
    order, at = [], 0
    for n in range(NU):
        order.append([("piece", at + j) for j in range(share[n])] + ([("turn", T_AT[n])] if n in T_AT else []))
        at += share[n]
    flat = [x for o in order for x in o]
    mx_use = {x: n for n, x in enumerate(flat)}
    mx_ring, sc_ring = Ring(MX, 2), Ring(SC, 4)
    PR = 3
    PUTS = 16 * 2 * HPG
    DIAG = [n for n, (c, i) in enumerate(units) if i >= BPH * c]

    ctx = ExitStack()
    with ctx:
        def sb(name, shape, dt=fp32):
            return ctx.enter_context(nc.sbuf_tensor(name, shape, dt))

        def sem(name):
            return ctx.enter_context(nc.semaphore(name))

        q3 = [sb(f"q3_{n}", [P, HPG, S], f32r) for n in range(SLOTS)]
        k3 = [sb(f"k3_{n}", [P, S], f32r) for n in range(SLOTS)]
        v = [sb(f"v_{n}", [P, QB, D]) for n in range(SLOTS)]
        probs = sb("probs", [P, PR, HPG, CH])
        rows_in = sb("rows_in", [P, HPG, S])
        distance = sb("distance", [P, S])
        ident = sb("ident2", [P, P])
        slope = sb("slope", [P, NH])
        ones = sb("ones", [P, D])
        credit = sb("credit2", [P, 6])
        unused = sb("unused", [P, 2, CH], bf16)
        mx = sb("mx", [P, 3 * BPH * HPG])
        mx1 = sb("mx1", [P, BPH * HPG])
        mxt_hi, mxt_lo = sb("mxt_hi", [BPH * HPG, HALF, P], f32r), sb("mxt_lo", [BPH * HPG, HALF, P], f32r)
        recip = sb("recip", [P, CH])
        att = sb("att", [P, HALF, CH])
        psum = [ctx.enter_context(nc.psum_tensor(f"pa{n}", [P, CH], fp32)) for n in range(8)]
        sc_ps, mx_ps, out_ps, sum_ps = psum[:4], psum[4:6], psum[6], psum[7]

        consts_in, rows_set, ones_set = sem("consts_in2"), sem("rows_set"), sem("ones_set")
        loaded = [sem(f"loaded{n}") for n in range(SLOTS)]
        neg_max = [[sem(f"neg_max{n}{c}") for c in range(HALF)] for n in range(SLOTS)]
        sc_done = sem("sc_done")
        mx_done, mx_free = sem("mx_done"), sem("mx_free")
        mx1_done = sem("mx1_done")
        mxt_hi_done = sem("mxt_hi_done")
        exp_done, cut_done = sem("exp_done"), sem("cut_done")
        pv_done, recip_done, att_done = sem("pv_done"), sem("recip_done"), sem("att_done")
        att_stored = [sem(f"att_stored{c}") for c in range(HALF)]
        block = ctx.enter_context(nc.Block())

        def piece_cols(p):
            return p if p < 16 else 16 + (p - 16) // 2 + 16 * ((p - 16) % 2)

        def load(sp, t, u):
            b, g = t // NG, t % NG
            tok = bass.ds(b * S, S)
            for row, half in ((0, q_hi_d), (D, q_hi_d), (2 * D, q_lo_d)):
                src = half[bass.ds(g, 1), :, tok].rearrange("g (h d) q -> d (g h) q", d=D)
                sp.dma_start(raw(q3[u][row:row + D, :, :]), src).then_inc(loaded[u], 16)
            sp.dma_start(raw(k3[u][0:3 * D, :]), k_d[:, tok]).then_inc(loaded[u], 16)
            sp.dma_start(v[u][:, :, :], v_d[:, bass.ds(b * QB, QB), :]).then_inc(loaded[u], 16)

        def put_max(sp, t, u, c):
            sp.wait_ge(mx_free, MX * t + MX + mx_use[("turn", c)] + 1)
            for row, half in ((3 * D + 2, mxt_hi), (3 * D + 3, mxt_lo)):
                for h in range(HPG):
                    sp.dma_start(raw(q3[u][row:row + 1, h, c * CH:(c + 1) * CH]), raw(half[h * BPH:(h + 1) * BPH, c, :])).then_inc(neg_max[u][c], 16)

        def put_att(sp, t, c):
            b, g = t // NG, t % NG
            sp.wait_ge(att_done, t * HALF + (c + 1) + CREDIT)
            sp.dma_start(att_d[bass.ds(g, 1), :, bass.ds(b * S + c * CH, CH)].rearrange("g p q -> p (g q)"), att[:, c, :]).then_inc(att_stored[c], 16)

        @block.sync
        def _(sp):
            sp.dma_start(rows_in[3 * D:KR, :, :], qrows_h[:, None, :].to_broadcast([KR - 3 * D, HPG, S])).then_inc(consts_in, 16)
            sp.dma_start(probs[3 * D:KR, 0, 0:2, :], krows_h.rearrange("r (a q) -> r a q", a=2)).then_inc(consts_in, 16)
            sp.dma_start(distance[:, :], distance_h).then_inc(consts_in, 16)
            sp.dma_start(ident[:, :], ident_h).then_inc(consts_in, 16)
            sp.dma_start(slope[:, :], slope_h).then_inc(consts_in, 16)
            load(sp, 0, 0)
            load(sp, 1, 1)
            put_max(sp, 0, 0, 0)
            put_max(sp, 0, 0, 1)

            def body(t, u, i):
                last, before_last = isinstance(t, int) and t == ITS - 1, isinstance(t, int) and t == ITS - 2
                if not last and not before_last:
                    sp.wait_ge(exp_done, t * EXPS + EXPS)
                    load(sp, t + 2, (u + 2) % SLOTS)
                put_att(sp, t, 0)
                if not last:
                    put_max(sp, t + 1, (u + 1) % SLOTS, 0)
                    put_max(sp, t + 1, (u + 1) % SLOTS, 1)
                put_att(sp, t, 1)

            run_loop(sp, ITS, SLOTS, body)
            for c in range(HALF):
                sp.wait_ge(att_stored[c], 16 * ITS + CREDIT)

        @block.gpsimd
        def _(pool):
            for n, (count, first) in enumerate(((mx_free, MX), (exp_done, EXPS), (pv_done, PR), (att_done, CREDIT),
                                                (att_stored[0], CREDIT), (att_stored[1], CREDIT))):
                pool.memset(credit[:, n:n + 1], 0.0).then_inc(count, first)
            pool.memset(ones[:, :], 1.0).then_inc(ones_set, 1)
            exps = Tally(pool, "exps", EXPS + HPG * (DIAG[0] + 1))

            def body(t, u, i):
                for d, n in enumerate(DIAG):
                    after = DIAG[d + 1] if d + 1 < len(DIAG) else NU + DIAG[0]
                    exps.wait(exp_done, t * EXPS + (EXPS + HPG * (n + 1)), HPG * (after - n))
                    block_of = probs[:, n % PR, :, 0:P]
                    nc.gpsimd.affine_select(out=block_of, in_=block_of, compare_op=ALU.is_ge, fill=0.0, base=0,
                                            pattern=[[0, HPG], [1, P]], channel_multiplier=-1).then_inc(cut_done, 1)

            run_loop(pool, ITS, SLOTS, body)

        @block.tensor
        def _(pe):
            def maxima_item(w, u, item):
                kind, m = item
                n = mx_use[item]
                pe.wait_ge(mx_free, mx_ring.free(w, n))
                bank = mx_ps[mx_ring.bank[n]]
                if kind == "piece":
                    _, h, qb, k0, keys = pieces[m]
                    nc.tensor.matmul(bank[:, 0:keys], q3[u][0:3 * D, h, qb * P:(qb + 1) * P], k3[u][0:3 * D, k0:k0 + keys],
                                     start=True, stop=True).then_inc(mx_done, 1)
                    return
                if m == 0:
                    pe.wait_ge(mx_free, w * MX + (MX + mx_use[("piece", 4 * HPG - 1)] + 1))
                    src = mx[:, 0:BPH * HPG]
                else:
                    pe.wait_ge(mx1_done, w + 1)
                    src = mx1[:, :]
                nc.tensor.transpose(bank[0:BPH * HPG, 0:P], src, ident[:, :]).then_inc(mx_done, 1)

            def scores(t, u, n):
                c, i = units[n]
                lo, N = span(units[n])
                heads = heads_at_once(units[n])
                for j in range(HPG // heads):
                    use = scores_of[n] + j
                    p = sc_ring.prev[use]
                    before = exps_through[p] if p >= 0 else exps_through[p + SC] - EXPS
                    pe.wait_ge(exp_done, t * EXPS + (EXPS + before))
                    bank = sc_ps[sc_ring.bank[use]][:, 0:heads * N].rearrange("p (h q) -> p h q", h=heads)
                    nc.tensor.matmul(bank, k3[u][0:KR, i * P:(i + 1) * P], q3[u][0:KR, j * heads:(j + 1) * heads, lo:lo + N],
                                     start=True, stop=True).then_inc(sc_done, 1)

            def values(t, u, n):
                c, i = units[n]
                lo, N = span(units[n])
                if n in DIAG:
                    pe.wait_ge(cut_done, t * len(DIAG) + DIAG.index(n) + 1)
                else:
                    pe.wait_ge(exp_done, t * EXPS + (EXPS + HPG * (n + 1)))
                if i == 0:
                    pe.wait_ge(att_done, t * HALF + c + CREDIT)
                for o, w in ((out_ps, v[u][:, i, :]), (sum_ps, ones[:, :])):
                    for h in range(HPG):
                        last = nc.tensor.matmul(o[h * D:(h + 1) * D, lo - c * CH:lo - c * CH + N], w, probs[:, n % PR, h, 0:N],
                                                start=(i == 0), stop=(i == BPH * (c + 1) - 1))
                last.then_inc(pv_done, 1)

            pe.wait_ge(consts_in, 16 * 5)
            pe.wait_ge(rows_set, 2 * SLOTS)
            pe.wait_ge(ones_set, 1)
            pe.wait_ge(loaded[0], 80)
            for item in flat:
                maxima_item(0, 0, item)

            def body(t, u, i):
                last = isinstance(t, int) and t == ITS - 1
                nu = (u + 1) % SLOTS
                if not last:
                    pe.wait_ge(loaded[nu], (i + (2 if nu == 0 else 1)) * 80)
                for n in range(NU):
                    items = [] if last else [x for x in order[n]]
                    tail = [x for x in items if x[0] == "turn"] if n == NU - 1 else []
                    items = [x for x in items if x not in tail]
                    for item in items[:2]:
                        maxima_item(t + 1, nu, item)
                    if n in (0, BPH):
                        pe.wait_ge(neg_max[u][n // BPH], (i + 1) * PUTS)
                    scores(t, u, n)
                    for item in items[2:]:
                        maxima_item(t + 1, nu, item)
                    if n:
                        values(t, u, n - 1)
                    if n == NU - 1:
                        values(t, u, n)
                    for item in tail:
                        maxima_item(t + 1, nu, item)

            run_loop(pe, ITS, SLOTS, body)

        @block.scalar
        def _(act):
            act.wait_ge(consts_in, 16 * 5)
            for n in range(SLOTS):
                nc.scalar.copy(q3[n][3 * D:KR, :, :], rows_in[3 * D:KR, :, :]).then_inc(rows_set, 1)
                nc.scalar.copy(k3[n][3 * D:KR, :].rearrange("r (a q) -> r a q", a=2),
                               probs[3 * D:KR, 0, 0:2, :]).then_inc(rows_set, 1)
            act.wait_ge(rows_set, 2 * SLOTS)
            scored = Tally(act, "scored", 1)

            def body(t, u, i):
                g = t % NG
                for n in range(NU):
                    _, N = span(units[n])
                    heads = heads_at_once(units[n])
                    act.wait_ge(pv_done, t * NU + (n + 1))
                    for h in range(HPG):
                        use = scores_of[n] + h // heads
                        if h % heads == 0:
                            scored.wait(sc_done, t * SC + (use + 1), 1)
                        at = (h % heads) * N
                        nc.scalar.activation(probs[:, n % PR, h, 0:N], sc_ps[sc_ring.bank[use]][:, at:at + N], ACT.Exp,
                                             scale=slope[:, bass.ds(g * HPG + h, 1)]).then_inc(exp_done, 1)

            run_loop(act, ITS, SLOTS, body)

        @block.vector
        def _(dve):
            dve.wait_ge(consts_in, 16 * 5)
            items_done = Tally(dve, "items_done", MX + 1)

            def reduce_item(w, pu, pi, item):
                kind, m = item
                n = mx_use[item]
                items_done.wait(mx_done, w * MX + (n + 1), 1)
                bank = mx_ps[mx_ring.bank[n]]
                if kind == "piece":
                    _, h, qb, k0, keys = pieces[m]
                    d0 = S - P - qb * P + k0
                    col = piece_cols(m)
                    nc.vector.tensor_tensor_reduce(out=unused[:, mx_ring.bank[n], 0:keys], in0=bank[:, 0:keys], in1=distance[:, d0:d0 + keys],
                                                   scale=1.0, scalar=-3e38, op0=ALU.add, op1=ALU.max,
                                                   accum_out=mx[:, col:col + 1]).then_inc(mx_free, 1)
                    if m == len(pieces) - 1:
                        dve.wait_ge(mx_free, w * MX + (MX + n + 1))
                        k = BPH * HPG
                        nc.vector.tensor_tensor(mx1[:, :], mx[:, k:2 * k], mx[:, 2 * k:3 * k], ALU.max).then_inc(mx1_done, 1)
                    return
                if pu is not None:
                    dve.wait_ge(neg_max[pu][m], (pi + 1) * PUTS)
                src = bank[0:BPH * HPG, 0:P]
                nc.vector.tensor_scalar(mxt_hi[:, m, :], src, -1.0, None, ALU.mult).then_inc(mxt_hi_done, 1)
                dve.wait_ge(mxt_hi_done, w * HALF + (m + 1))
                nc.vector.scalar_tensor_tensor(out=mxt_lo[:, m, :], in0=src, scalar=-1.0, in1=raw(mxt_hi[:, m, :]),
                                               op0=ALU.mult, op1=ALU.subtract).then_inc(mx_free, 1)

            def normalize(t, c):
                dve.wait_ge(pv_done, t * NU + (PR + BPH * (1 if c == 0 else 3)))
                nc.vector.reciprocal(recip[:, :], sum_ps[:, :]).then_inc(recip_done, 1)
                dve.wait_ge(recip_done, t * HALF + (c + 1))
                dve.wait_ge(att_stored[c], t * 16 + CREDIT)
                nc.vector.tensor_tensor(att[:, c, :], out_ps[:, :], recip[:, :], ALU.mult).then_inc(att_done, 1)

            for item in flat:
                reduce_item(0, None, None, item)

            def body(t, u, i):
                last = isinstance(t, int) and t == ITS - 1
                for n in range(NU):
                    items = [] if last else order[n]
                    tail = [x for x in items if x[0] == "turn"] if n == NU - 1 else []
                    for item in items:
                        if item not in tail:
                            reduce_item(t + 1, u, i, item)
                    if n == BPH:
                        normalize(t, 0)
                    if n == NU - 1:
                        normalize(t, 1)
                    for item in tail:
                        reduce_item(t + 1, u, i, item)

            run_loop(dve, ITS, SLOTS, body)


def finish(nc, x, bias_h, ident_h, att_d, wo_d, wf_d, out):
    NT = T // P
    x_v = x.rearrange("b s h -> (b s) h").rearrange("(t p) h -> p t h", p=P)
    out_v = out.rearrange("b s h -> (b s) h").rearrange("(t p) h -> p t h", p=P)
    HV = H // CH
    LSTEPS = 8

    ctx = ExitStack()
    with ctx:
        def sb(name, shape, dt=fp32):
            return ctx.enter_context(nc.sbuf_tensor(name, shape, dt))

        def sem(name):
            return ctx.enter_context(nc.semaphore(name))

        wo_hi, wo_lo = sb("fo_hi", [P, KT, H], f32r), sb("fo_lo", [P, KT, H], f32r)
        wf_hi, wf_lo = sb("ff_hi", [P, KT, H], f32r), sb("ff_lo", [P, KT, H], f32r)
        at_in = sb("at_in", [P, KT, P])
        at_hi, at_lo = sb("at_hi", [P, 2, KT, P], f32r), sb("at_lo", [P, 2, KT, P], f32r)
        x_in = sb("x3_in", [P, 2, H])
        y = sb("y", [P, 2, H])
        yb = sb("yb", [P, H])
        yt_hi, yt_lo = sb("yt_hi", [P, KT, P], f32r), sb("yt_lo", [P, KT, P], f32r)
        z = sb("z", [P, 2, H])
        bias, credit = sb("bias", [P, H]), sb("credit3", [P, 2])
        ident = sb("ident3", [P, P])
        stats = [sb(f"stats{n}", [P, HV, 6]) for n in range(2)]
        mv = [sb(f"mv{n}", [P, 2]) for n in range(2)]
        var_eps, std, rstd0, ratio, fix, rstd = ([sb(f"ln{k}{n}", [P, 1]) for n in range(2)] for k in range(6))
        psum = [ctx.enter_context(nc.psum_tensor(f"pf{n}", [P, CH], fp32)) for n in range(6)]
        o_ps, f_ps, t_ps = psum[0:2], psum[2:4], psum[4:6]

        consts_in, wo_in, wf_in = sem("consts_in3"), sem("wo_in"), sem("wf_in")
        at_loaded, x_loaded = sem("at_loaded"), [sem(f"x3_loaded{n}") for n in range(2)]
        at_hi_done, at_lo_done = sem("at_hi_done"), sem("at_lo_done")
        o_done, y_sum, ln_steps = sem("o_done"), sem("y_sum"), [sem(f"ln_steps{n}") for n in range(2)]
        std_done = [sem(f"std_done{n}") for n in range(2)]
        yb_done, yt_turned, yt_hi_done, yt_lo_done = sem("yb_done"), sem("yt_turned"), sem("yt_hi_done"), sem("yt_lo_done")
        f_done, z_sum, stored = sem("f_done"), sem("z_sum"), [sem(f"stored{n}") for n in range(2)]
        block = ctx.enter_context(nc.Block())

        @block.sync
        def _(sp):
            sp.dma_start(bias[:, :], bias_h[None, :].to_broadcast([P, H])).then_inc(consts_in, 16)
            sp.dma_start(ident[:, :], ident_h).then_inc(consts_in, 16)
            def load(t, u):
                sp.dma_start(at_in[:, :, :], att_d[:, :, bass.ds(t * P, P)].rearrange("g p q -> p g q")).then_inc(at_loaded, 16)
                sp.dma_start(x_in[:, u:u + 1, :], x_v[:, bass.ds(t, 1), :]).then_inc(x_loaded[u], 16)
            load(0, 0)
            for n, w in enumerate((wo_hi, wo_lo)):
                sp.dma_start(raw(w[:, :, :]), wo_d[n]).then_inc(wo_in, 16)
            for n, w in enumerate((wf_hi, wf_lo)):
                sp.dma_start(raw(w[:, :, :]), wf_d[n]).then_inc(wf_in, 16)

            def body(t, u, i):
                first, last = isinstance(t, int) and t == 0, isinstance(t, int) and t == NT - 1
                if not last:
                    sp.wait_ge(at_lo_done, t + 1)
                    load(t + 1, 1 - u)
                if not first and not (isinstance(t, int) and t == 1):
                    store(t - 2, u)

            def store(t, u):
                sp.wait_ge(ln_steps[1], t * LSTEPS + LSTEPS)
                sp.dma_start(out_v[:, bass.ds(t, 1), :], z[:, u:u + 1, :]).then_inc(stored[u], 16)

            edge_loop(sp, NT, body)
            store(NT - 2, 0)
            store(NT - 1, 1)
            for u in range(2):
                sp.wait_ge(stored[u], NT // 2 * 16 + CREDIT)

        @block.tensor
        def _(pe):
            def product(ps, done, lhs, rhs, h):
                for k in range(KT):
                    for n, (a, w) in enumerate(((lhs[0], rhs[0]), (lhs[0], rhs[1]), (lhs[1], rhs[0]))):
                        last = nc.tensor.matmul(ps[h][:, :], a[:, k, :], w[:, k, h * CH:(h + 1) * CH],
                                                start=(k == 0 and n == 0), stop=(k == KT - 1 and n == 2))
                last.then_inc(done, 1)

            def linear(t, u):
                pe.wait_ge(yt_lo_done, t * 2 + 2)
                pe.wait_ge(z_sum, t * HV)
                if isinstance(t, int) and t == 0:
                    pe.wait_ge(wf_in, 32)
                for h in range(HV):
                    product(f_ps, f_done, (yt_hi, yt_lo), (wf_hi, wf_lo), h)

            def turn(t, u):
                pe.wait_ge(ln_steps[0], t * LSTEPS + LSTEPS)
                pe.wait_ge(yt_lo_done, t * 2)
                for j in range(2):
                    for k in range(4):
                        cols = slice((j * 4 + k) * P, (j * 4 + k + 1) * P)
                        last = nc.tensor.transpose(t_ps[j][:, k * P:(k + 1) * P], y[:, u, cols], ident[:, :])
                    last.then_inc(yt_turned, 1)

            pe.wait_ge(consts_in, 32)
            pe.wait_ge(wo_in, 32)

            def body(t, u, i):
                first = isinstance(t, int) and t == 0
                pe.wait_ge(at_lo_done, t + 1)
                pe.wait_ge(y_sum, t * HV)
                at = (at_hi[:, u, :, :], at_lo[:, u, :, :])
                product(o_ps, o_done, at, (wo_hi, wo_lo), 0)
                if not first:
                    turn(t - 1, 1 - u)
                product(o_ps, o_done, at, (wo_hi, wo_lo), 1)
                if not first:
                    linear(t - 1, 1 - u)

            edge_loop(pe, NT, body)
            turn(NT - 1, (NT - 1) % 2)
            linear(NT - 1, (NT - 1) % 2)

        @block.scalar
        def _(act):
            def split_hi(t, u, first=False):
                act.wait_ge(at_loaded, t * 16 + 16)
                if not first:
                    act.wait_ge(o_done, (t - 1) * HV)
                nc.scalar.copy(at_hi[:, u, :, :], at_in[:, :, :]).then_inc(at_hi_done, 1)

            def root(t, which):
                act.wait_ge(ln_steps[which], t * LSTEPS + 3)
                nc.scalar.activation(std[which][:, :], var_eps[which][:, :], ACT.Sqrt).then_inc(std_done[which], 1)

            def turned_hi(t, first=False):
                if not first:
                    act.wait_ge(f_done, t * HV)
                for j in range(2):
                    act.wait_ge(yt_turned, t * 2 + (j + 1))
                    nc.scalar.copy(yt_hi[:, j * 4:j * 4 + 4, :], t_ps[j][:, :].rearrange("p (k q) -> p k q", q=P)).then_inc(yt_hi_done, 1)

            split_hi(0, 0, True)

            def body(t, u, i):
                first, second = (isinstance(t, int) and t == n for n in (0, 1))
                last = isinstance(t, int) and t == NT - 1
                if not first and not second:
                    root(t - 2, 1)
                if not first:
                    turned_hi(t - 1)
                if not last:
                    split_hi(t + 1, 1 - u, first)
                root(t, 0)

            edge_loop(act, NT, body)
            root(NT - 2, 1)
            turned_hi(NT - 1)
            root(NT - 1, 1)

        @block.gpsimd
        def _(pool):
            for u in range(2):
                pool.memset(credit[:, u:u + 1], 0.0).then_inc(stored[u], CREDIT)
            pool.wait_ge(consts_in, 32)

            def add_bias(t, u):
                pool.wait_ge(ln_steps[0], t * LSTEPS + LSTEPS)
                pool.wait_ge(z_sum, t * HV)
                nc.gpsimd.tensor_tensor(yb[:, :], y[:, u, :], bias[:, :], ALU.add).then_inc(yb_done, 1)

            def body(t, u, i):
                add_bias(t, u)

            edge_loop(pool, NT, body)

        @block.vector
        def _(dve):
            def split_lo(t, u):
                dve.wait_ge(at_hi_done, t + 1)
                nc.vector.tensor_tensor(at_lo[:, u, :, :], at_in[:, :, :], raw(at_hi[:, u, :, :]),
                                        ALU.subtract).then_inc(at_lo_done, 1)

            def sum_and_stats(t, u, which, h):
                done, ps, other, to, sums = ((o_done, o_ps, x_in[:, u, :], y, y_sum), (f_done, f_ps, yb, z, z_sum))[which]
                cols = slice(h * CH, (h + 1) * CH)
                dve.wait_ge(done, t * HV + (h + 1))
                nc.vector.tensor_tensor(to[:, u, cols], ps[h][:, :], other[:, cols], ALU.add).then_inc(sums, 1)
                dve.wait_ge(sums, t * HV + (h + 1))
                ins = nc.vector.bn_stats(stats[which][:, h, :], to[:, u, cols])
                if h == HV - 1:
                    ins.then_inc(ln_steps[which], 1)

            def norm(t, u, which):
                w, to = which, (y, z)[which]
                steps = [1]

                def step(ins):
                    steps[0] += 1
                    ins.then_inc(ln_steps[w], 1)
                    if steps[0] < LSTEPS:
                        dve.wait_ge(ln_steps[w], t * LSTEPS + steps[0])

                stats_done[w].wait(ln_steps[w], t * LSTEPS + 1, LSTEPS)
                step(nc.vector.bn_aggr(mv[w][:, :], stats[w][:, :, :]))
                step(nc.vector.tensor_scalar(var_eps[w][:, :], mv[w][:, 1:2], EPS, None, ALU.add))
                dve.wait_ge(std_done[w], t + 1)
                step(nc.vector.reciprocal(rstd0[w][:, :], std[w][:, :]))
                step(nc.vector.scalar_tensor_tensor(out=ratio[w][:, :], in0=rstd0[w][:, :], scalar=rstd0[w][:, :],
                                                    in1=var_eps[w][:, :], op0=ALU.mult, op1=ALU.mult))
                step(nc.vector.tensor_scalar(fix[w][:, :], ratio[w][:, :], -0.5, 1.5, ALU.mult, ALU.add))
                step(nc.vector.tensor_tensor(rstd[w][:, :], rstd0[w][:, :], fix[w][:, :], ALU.mult))
                step(nc.vector.tensor_scalar(to[:, u, :], to[:, u, :], mv[w][:, 0:1], rstd[w][:, :], ALU.subtract, ALU.mult))
                assert steps[0] == LSTEPS

            def turned_lo(t):
                if not (isinstance(t, int) and t == 0):
                    dve.wait_ge(f_done, t * HV)
                for j in range(2):
                    dve.wait_ge(yt_hi_done, t * 2 + (j + 1))
                    nc.vector.tensor_tensor(yt_lo[:, j * 4:j * 4 + 4, :], t_ps[j][:, :].rearrange("p (k q) -> p k q", q=P),
                                            raw(yt_hi[:, j * 4:j * 4 + 4, :]), ALU.subtract).then_inc(yt_lo_done, 1)

            def z_half(t, u, i, h):
                if h == 0:
                    dve.wait_ge(yb_done, t + 1)
                    dve.wait_ge(stored[u], i * 16 + CREDIT)
                sum_and_stats(t, u, 1, h)

            stats_done = [Tally(dve, f"stats_done{n}", first * LSTEPS + 1) for n, first in enumerate((2, 0))]
            split_lo(0, 0)

            def body(t, u, i):
                first, second = (isinstance(t, int) and t == n for n in (0, 1))
                last = isinstance(t, int) and t == NT - 1
                if not first and not second:
                    z_half(t - 2, u, i - 1, 1)
                    norm(t - 2, u, 1)
                    dve.wait_ge(yt_turned, (t - 1) * 2)
                    dve.wait_ge(yb_done, t - 1)
                dve.wait_ge(x_loaded[u], i * 16 + 16)
                sum_and_stats(t, u, 0, 0)
                if not first:
                    turned_lo(t - 1)
                sum_and_stats(t, u, 0, 1)
                norm(t, u, 0)
                if not last:
                    split_lo(t + 1, 1 - u)
                if not first:
                    z_half(t - 1, 1 - u, i if u == 1 else i - 1, 0)

            edge_loop(dve, NT, body)
            z_half(NT - 2, 0, NT // 2 - 1, 1)
            norm(NT - 2, 0, 1)
            turned_lo(NT - 1)
            z_half(NT - 1, 1, NT // 2 - 1, 0)
            z_half(NT - 1, 1, NT // 2 - 1, 1)
            norm(NT - 1, 1, 1)


_INS = ["L0_attn_hidden_states", "L0_attn_Wqkv", "L0_attn_Wo", "L0_ffn_weight", "L0_ffn_bias"]
_CONSTS = ["c_qscale", "c_distance", "c_qrows", "c_krows", "c_ident", "c_slope"]


def kernel(**inputs):
    import numpy as _np
    import concourse.bacc as _bacc
    from concourse import mybir as _mybir
    from concourse.bass_utils import run_bass_kernel_spmd as _run

    nc = _bacc.Bacc("TRN2", target_bir_lowering=False, num_devices=1)
    consts = shape_constants()
    arrays, args = {}, []
    for name in _INS + _CONSTS:
        a = _np.ascontiguousarray(inputs[name] if name in inputs else consts[name])
        arrays[f"in_{name}"] = a
        args.append(nc.dram_tensor(f"in_{name}", a.shape, _mybir.dt.from_np(a.dtype), kind="ExternalInput").ap())
    result = nc.dram_tensor("out_0", (B, S, H), _mybir.dt.float32, kind="ExternalOutput").ap()
    layer(nc, *args, result)
    r = _run(nc, [arrays], core_ids=[0])
    return r.results[0]["out_0"]
```

```python
import concourse.bass as bass
from concourse import mybir
from contextlib import ExitStack
import numpy as np

P = 128
B, S, H = 4, 1024, 1024
NH, D = 32, 32
T = B * S
KT = H // P
HPG = P // D
NG = NH // HPG
CH = 512
NCH = T // CH
QKV = NH * D + 2 * D
EPS = 1e-5
QMAX, QMIN = 7.0, -8.0
ROUND = 1.5 * 2.0 ** 23
MASKED = -1e30
SPANS = 16
CREDIT = 16

fp32 = mybir.dt.float32
f32r = mybir.dt.float32r
bf16 = mybir.dt.bfloat16
ALU = mybir.AluOpType
ACT = mybir.ActivationFunctionType
AXX = mybir.AxisListType.X


def slopes():
    base = 2.0 ** (-2.0 ** (-(np.log2(NH) - 3)))
    return (base ** np.arange(1, NH + 1, dtype=np.float64)).astype(np.float32)


def shape_constants():
    sl = slopes()
    head = np.arange(NG)[None, :] * HPG + np.arange(P)[:, None] // D
    qscale = (np.float64(D) ** -0.5 / sl.astype(np.float64)[head]).astype(np.float32)
    rel = np.arange(S)[None, :] - (S - P) - np.arange(P)[:, None]
    distance = np.where(rel <= 0, rel, MASKED).astype(np.float32)
    pos, starts = np.arange(S), np.arange(SPANS)[:, None] * (S // SPANS)
    q_rows = np.concatenate([[np.ones(S), -pos, np.zeros(S), np.zeros(S)], np.where(pos < starts, MASKED, 0.0)])
    k_rows = np.concatenate([[pos, np.ones(S), np.ones(S), np.ones(S)], (pos >= starts) & (pos < starts + S // SPANS)])
    q_rows, k_rows = q_rows.astype(np.float32), k_rows.astype(np.float32)
    slope = np.broadcast_to(sl[None, :], (P, NH)).astype(np.float32)
    return {"c_qscale": qscale, "c_distance": distance, "c_qrows": q_rows, "c_krows": k_rows,
            "c_ident": np.eye(P, dtype=np.float32), "c_slope": np.ascontiguousarray(slope)}


class Tally:
    def __init__(self, eng, name, first):
        self.eng, self.reg = eng, eng.alloc_register(name)
        eng.reg_mov(self.reg, first)

    def wait(self, sem, value, to_next):
        if isinstance(value, int):
            self.eng.wait_ge(sem, value)
        else:
            self.eng.wait_ge(sem, self.reg)
            self.eng.reg_add(self.reg, self.reg, to_next)


def raw(ap):
    return ap.bitcast(fp32)


def run_loop(eng, total, unroll, body):
    trips = (total - 1) // unroll
    with eng.Fori(0, trips) as i:
        for u in range(unroll):
            body(i * unroll + u, u, i)
    for t in range(trips * unroll, total):
        body(t, t % unroll, t // unroll)


def edge_loop(eng, total, body):
    for t in range(2):
        body(t, t, 0)
    with eng.Fori(1, total // 2 - 1) as i:
        for u in range(2):
            body(i * 2 + u, u, i)
    for t in range(total - 2, total):
        body(t, t % 2, t // 2)


def slot_loop(eng, total, unroll, body):
    body(0, 0, 0)
    trips = (total - 3) // unroll
    with eng.Fori(0, trips) as j:
        for w in range(1, unroll + 1):
            body(j * unroll + w, w % unroll, j + w // unroll)
    for t in range(trips * unroll + 1, total):
        body(t, t % unroll, t // unroll)


class Ring:
    def __init__(self, K, banks):
        self.K = K
        self.bank = [n % banks for n in range(K)]
        self.prev = []
        for n in range(K):
            before = [m for m in range(n) if self.bank[m] == self.bank[n]]
            last = [m - K for m in range(K) if self.bank[m] == self.bank[n]]
            self.prev.append(before[-1] if before else last[-1])

    def free(self, t, n):
        return t * self.K + (self.K + self.prev[n] + 1)


def layer(nc, x, wqkv, wo, wf, bias, qscale, distance, qrows, krows, ident_h, slope_h, out):
    def dram(name, shape, dt):
        return nc.dram_tensor(name, shape, dt, kind="Internal").ap()

    q_hi_d = dram("q_hi_d", [NG, P, T], fp32)
    q_lo_d = dram("q_lo_d", [NG, P, T], fp32)
    k_d = dram("k_d", [3 * D, T], fp32)
    v_d = dram("v_d", [P, T // P, D], fp32)
    att_d = dram("att_d", [NG, P, T], fp32)
    sums_d = dram("sums_d", [B * NG, HPG, S], fp32)
    recip_d = dram("recip_d", [B * NG, HPG, S], fp32)
    wo_d = dram("wo_d", [2, P, KT, H], fp32)
    wf_d = dram("wf_d", [2, P, KT, H], fp32)
    project(nc, x, wqkv, wo, wf, qscale, ident_h, q_hi_d, q_lo_d, k_d, v_d, wo_d, wf_d)
    with ExitStack() as ctx:
        w3 = [ctx.enter_context(nc.sbuf_tensor(n, [P, KT, H], f32r)) for n in ("fo_hi", "fo_lo", "ff_hi")]
        w3_in = [ctx.enter_context(nc.semaphore(n)) for n in ("fo_hi_in", "fo_lo_in", "ff_hi_in")]
        attend(nc, distance, qrows, krows, ident_h, slope_h, q_hi_d, q_lo_d, k_d, v_d, att_d, sums_d, recip_d,
               wo_d, wf_d, w3, w3_in)
        finish(nc, x, bias, ident_h, att_d, recip_d, wf_d, w3, w3_in, out)


def project(nc, x, wqkv, wo, wf, qscale_h, ident_h, q_hi_d, q_lo_d, k_d, v_d, wo_d, wf_d):
    x_v = x.rearrange("b s h -> (b s) h").rearrange("(c s p) h -> p c s h", p=P, s=CH // P)
    SUB = CH // P
    QC = NG
    MM = QC + 1
    TR = KT + 2 + 1
    mm_ring, tr_ring = Ring(MM, 4), Ring(TR, 4)
    TR_V, TR_X, TR_W = 0, 1, 1 + KT
    SCALE_STEPS, QUOT_STEPS = 12, 12
    QSTEPS = SCALE_STEPS + 2 * QUOT_STEPS + 5

    ctx = ExitStack()
    with ctx:
        def sb(name, shape, dt=fp32):
            return ctx.enter_context(nc.sbuf_tensor(name, shape, dt))

        def sem(name):
            return ctx.enter_context(nc.semaphore(name))

        wq_hi, wq_lo = sb("wq_hi", [P, KT, QKV], f32r), sb("wq_lo", [P, KT, QKV], f32r)
        x_in = sb("x_in", [P, SUB, H])
        xt_hi, xt_lo = sb("xt_hi", [P, 2, KT, CH], f32r), sb("xt_lo", [P, 2, KT, CH], f32r)
        stage = sb("stage", [P, 4, QKV])
        q_hi, q_lo = sb("q_hi", [P, 2, CH], f32r), sb("q_lo", [P, 2, CH], f32r)
        k_hi, k_lo = sb("k_hi", [D, CH], f32r), sb("k_lo", [D, CH], f32r)
        vt = sb("vt", [D, CH])
        v_sb = sb("v_sb", [P, SUB, D])
        wf_hi, wf_lo = sb("wf_hi", [P, KT, P], f32r), sb("wf_lo", [P, KT, P], f32r)
        wo_hi, wo_lo = sb("wo_hi", [P, H], f32r), sb("wo_lo", [P, H], f32r)
        ident = sb("ident1", [P, P])
        qscale = sb("qscale", [P, NG])
        seven, credit = sb("seven", [P, KT]), sb("credit", [P, 6])
        top, low, absmax, scale, isz, safe, scale0, rest, inv, half_lo = (sb(f"quant{n}", [P, KT]) for n in range(10))
        half_hi = sb("half_hi", [P, KT], f32r)
        quot_hi, quot_lo, part = sb("quot_hi", [P, KT // 2, P], f32r), sb("quot_lo", [P, KT // 2, P]), sb("part", [P, KT // 2, P])
        psum = [ctx.enter_context(nc.psum_tensor(f"ps{n}", [P, CH], fp32)) for n in range(8)]
        mm_ps, tr_ps = psum[:4], psum[4:]

        consts_in = sem("consts_in")
        wq_in = [sem(f"wq_in{n}") for n in range(4)]
        wq_hi_done, wq_lo_done = sem("wq_hi_done"), sem("wq_lo_done")
        x_loaded = sem("x_loaded")
        tr_done, tr_hi, tr_free = sem("tr_done"), sem("tr_hi"), sem("tr_free")
        mm_done, mm_hi, mm_free = sem("mm_done"), sem("mm_hi"), sem("mm_free")
        q_stored = [sem(f"q_stored{n}") for n in range(2)]
        kv_stored, vt_ready = sem("kv_stored"), sem("vt_ready")
        w_loaded, wo_loaded = sem("w_loaded"), sem("wo_loaded")
        quant_steps = sem("quant_steps")
        wo_hi_done, wo_lo_done = sem("wo_hi_done"), sem("wo_lo_done")
        wf_stored, wo_stored = sem("wf_stored"), sem("wo_stored")
        block = ctx.enter_context(nc.Block())

        w_blk = wf.rearrange("(t p) i -> p t i", p=P)
        wo_blk = wo.rearrange("(t p) o -> p t o", p=P)
        W_STAGE, WO_STAGE = 0, 3

        def tr_uses(t, n):
            skipped = KT if isinstance(t, int) and t == NCH - 1 and n >= TR_W else 0
            return t * TR + (KT + n + 1 - skipped)

        def tr_freed(t, n):
            return tr_uses(t, n) + TR

        @block.sync
        def _(sp):
            sp.dma_start(ident[:, :], ident_h).then_inc(consts_in, 16)
            sp.dma_start(qscale[:, :], qscale_h).then_inc(consts_in, 16)
            sp.dma_start(x_in[:, :, :], x_v[:, 0, :, :]).then_inc(x_loaded, 16)
            for k in range(KT):
                if k >= 4:
                    sp.wait_ge(wq_hi_done, k - 3)
                    sp.wait_ge(wq_lo_done, k - 3)
                sp.dma_start(stage[:, k % 4, :], wqkv[k * P:(k + 1) * P, :]).then_inc(wq_in[k % 4], 16)
            sp.wait_ge(tr_done, KT)
            sp.dma_start(x_in[:, :, :], x_v[:, 1, :, :]).then_inc(x_loaded, 16)
            sp.wait_ge(wq_hi_done, KT)
            sp.wait_ge(wq_lo_done, KT)
            sp.dma_start(stage[:, W_STAGE, 0:H], w_blk[:, 0, :]).then_inc(w_loaded, 16)
            sp.dma_start(stage[:, WO_STAGE, 0:H], wo_blk[:, 0, :]).then_inc(wo_loaded, 16)

            def body(t, u, i):
                last, before_last = isinstance(t, int) and t == NCH - 1, isinstance(t, int) and t == NCH - 2
                tok = bass.ds(t * CH, CH)
                sp.wait_ge(mm_free, t * MM + MM + 1)
                for row, half in ((0, k_hi), (D, k_lo), (2 * D, k_hi)):
                    sp.dma_start(k_d[row:row + D, tok], raw(half[:, :])).then_inc(kv_stored, 16)
                sp.wait_ge(wo_lo_done, t + 1)
                for n, half in enumerate((wo_hi, wo_lo)):
                    sp.dma_start(wo_d[n, :, bass.ds(t, 1), :], raw(half[:, :])[:, None, :]).then_inc(wo_stored, 16)
                if not last:
                    sp.dma_start(stage[:, WO_STAGE:WO_STAGE + 1, 0:H], wo_blk[:, bass.ds(t + 1, 1), :]).then_inc(wo_loaded, 16)
                for c in range(QC):
                    sp.wait_ge(mm_free, t * MM + MM + 2 + c)
                    sp.dma_start(q_hi_d[c, :, tok], raw(q_hi[:, c % 2, :])).then_inc(q_stored[c % 2], 16)
                    sp.dma_start(q_lo_d[c, :, tok], raw(q_lo[:, c % 2, :])).then_inc(q_stored[c % 2], 16)
                    if c == 1:
                        sp.wait_ge(tr_free, tr_freed(t, TR_V))
                        sp.dma_start(v_d[:, bass.ds(t * SUB, SUB), :], v_sb[:, :, :]).then_inc(kv_stored, 16)
                    if c == 5 and not last and not before_last:
                        sp.wait_ge(tr_done, tr_uses(t, TR_X + KT - 1))
                        sp.dma_start(x_in[:, None, :, :], x_v[:, bass.ds(t + 2, 1), :, :]).then_inc(x_loaded, 16)
                sp.wait_ge(tr_free, tr_freed(t, TR_W + 1))
                for n, half in enumerate((wf_hi, wf_lo)):
                    sp.dma_start(wf_d[n, :, :, bass.ds(t * P, P)], raw(half[:, :, :])).then_inc(wf_stored, 16)
                if not last:
                    sp.dma_start(stage[:, W_STAGE:W_STAGE + 1, 0:H], w_blk[:, bass.ds(t + 1, 1), :]).then_inc(w_loaded, 16)

            run_loop(sp, NCH, 2, body)
            for n in range(2):
                sp.wait_ge(q_stored[n], NCH * QC // 2 * 32 + CREDIT)
            sp.wait_ge(kv_stored, NCH * 64 + CREDIT)
            sp.wait_ge(wo_stored, NCH * 32 + CREDIT)
            sp.wait_ge(wf_stored, NCH * 32 + CREDIT)

        @block.gpsimd
        def _(pool):
            pool.memset(seven[:, :], QMAX).then_inc(tr_free, TR)
            pool.memset(credit[:, 0:1], 0.0).then_inc(mm_free, MM)
            for n, stored in enumerate((kv_stored, wo_stored, wf_stored, q_stored[0], q_stored[1])):
                pool.memset(credit[:, n + 1:n + 2], 0.0).then_inc(stored, CREDIT)

        @block.tensor
        def _(pe):
            def product(t, u, c):
                pe.wait_ge(mm_free, mm_ring.free(t, c))
                cols = slice(NH * D, QKV) if c == 0 else slice((c - 1) * P, c * P)
                o = mm_ps[mm_ring.bank[c]][0:cols.stop - cols.start, :]
                for k in range(KT):
                    for n, (w, xt) in enumerate(((wq_hi, xt_hi), (wq_hi, xt_lo), (wq_lo, xt_hi))):
                        last = nc.tensor.matmul(o, w[:, k, cols], xt[:, u, k, :], start=(k == 0 and n == 0),
                                                stop=(k == KT - 1 and n == 2))
                last.then_inc(mm_done, 1)

            def transpose_x(bank, k):
                for s in range(SUB):
                    last = nc.tensor.transpose(bank[:, s * P:(s + 1) * P], x_in[:, s, k * P:(k + 1) * P], ident[:, :])
                last.then_inc(tr_done, 1)

            v_chunks = Tally(pe, "v_chunks", 1)
            pe.wait_ge(consts_in, 32)
            pe.wait_ge(x_loaded, 16)
            for k in range(KT):
                if k >= 4:
                    pe.wait_ge(tr_free, TR + k - 3)
                transpose_x(tr_ps[k % 4], k)
            pe.wait_ge(wq_lo_done, KT)
            pe.wait_ge(tr_free, TR + KT)

            def body(t, u, i):
                last = isinstance(t, int) and t == NCH - 1
                pe.wait_ge(tr_free, t * TR + (KT + TR_X + KT))
                for c in range(MM):
                    product(t, u, c)
                    if c == 1:
                        pe.wait_ge(tr_free, KT + tr_ring.free(t, TR_V))
                        v_chunks.wait(vt_ready, t + 1, 1)
                        bank = tr_ps[tr_ring.bank[TR_V]]
                        for s in range(SUB):
                            done = nc.tensor.transpose(bank[:, s * D:(s + 1) * D], vt[:, s * P:(s + 1) * P], ident[0:D, 0:D])
                        done.then_inc(tr_done, 1)
                    if c == 3 and not last:
                        pe.wait_ge(x_loaded, t * 16 + 32)
                    if 3 <= c <= 6 and not last:
                        for k in (2 * (c - 3), 2 * (c - 3) + 1):
                            pe.wait_ge(tr_free, KT + tr_ring.free(t, TR_X + k))
                            transpose_x(tr_ps[tr_ring.bank[TR_X + k]], k)
                    if c == 7:
                        pe.wait_ge(quant_steps, t * QSTEPS + QSTEPS)
                        for h in range(2):
                            pe.wait_ge(tr_free, tr_freed(t, TR_W + h) - 1 - h if last else KT + tr_ring.free(t, TR_W + h))
                            bank = tr_ps[tr_ring.bank[TR_W + h]]
                            for j in range(4):
                                i = h * 4 + j
                                done = nc.tensor.transpose(bank[:, j * P:(j + 1) * P], stage[:, 2, i * P:(i + 1) * P], ident[:, :])
                            done.then_inc(tr_done, 1)

            run_loop(pe, NCH, 2, body)

        @block.scalar
        def _(act):
            act.wait_ge(consts_in, 32)
            for k in range(KT):
                act.wait_ge(tr_done, k + 1)
                nc.scalar.copy(xt_hi[:, 0, k, :], tr_ps[k % 4][:, :]).then_inc(tr_hi, 1)
            for k in range(KT):
                act.wait_ge(wq_in[k % 4], 16 * (k // 4 + 1))
                nc.scalar.copy(wq_hi[:, k, :], stage[:, k % 4, :]).then_inc(wq_hi_done, 1)

            def body(t, u, i):
                last = isinstance(t, int) and t == NCH - 1
                act.wait_ge(wo_loaded, t * 16 + 16)
                act.wait_ge(wo_stored, t * 32 + CREDIT)
                nc.scalar.copy(wo_hi[:, :], stage[:, WO_STAGE, 0:H]).then_inc(wo_hi_done, 1)
                for c in range(MM):
                    act.wait_ge(mm_done, t * MM + c + 1)
                    bank = mm_ps[mm_ring.bank[c]]
                    if c == 0:
                        act.wait_ge(kv_stored, t * 64 + CREDIT)
                        nc.scalar.copy(vt[:, :], bank[D:2 * D, :]).then_inc(vt_ready, 1)
                        nc.scalar.copy(k_hi[:, :], bank[0:D, :]).then_inc(mm_hi, 1)
                    else:
                        act.wait_ge(q_stored[(c - 1) % 2], t * (32 * QC // 2) + 32 * ((c - 1) // 2) + CREDIT)
                        nc.scalar.activation(q_hi[:, (c - 1) % 2, :], bank[:, :], ACT.Copy,
                                             scale=qscale[:, c - 1:c]).then_inc(mm_hi, 1)
                    if 3 <= c <= 6 and not last:
                        for k in (2 * (c - 3), 2 * (c - 3) + 1):
                            act.wait_ge(tr_done, tr_uses(t, TR_X + k))
                            nc.scalar.copy(xt_hi[:, 1 - u, k, :], tr_ps[tr_ring.bank[TR_X + k]][:, :]).then_inc(tr_hi, 1)
                    if c == 7:
                        act.wait_ge(wf_stored, t * 32 + CREDIT)
                        for h in range(2):
                            act.wait_ge(tr_done, tr_uses(t, TR_W + h))
                            nc.scalar.copy(wf_hi[:, h * 4:h * 4 + 4, :], tr_ps[tr_ring.bank[TR_W + h]][:, :]
                                           .rearrange("p (j o) -> p j o", o=P)).then_inc(tr_hi, 1)

            run_loop(act, NCH, 2, body)

        @block.vector
        def _(dve):
            for k in range(KT):
                dve.wait_ge(tr_hi, k + 1)
                nc.vector.tensor_tensor(xt_lo[:, 0, k, :], tr_ps[k % 4][:, :], raw(xt_hi[:, 0, k, :]),
                                        ALU.subtract).then_inc(tr_free, 1)
            for k in range(KT):
                dve.wait_ge(wq_hi_done, k + 1)
                nc.vector.tensor_tensor(wq_lo[:, k, :], stage[:, k % 4, :], raw(wq_hi[:, k, :]),
                                        ALU.subtract).then_inc(wq_lo_done, 1)

            w = stage[:, W_STAGE, 0:H].rearrange("p (g i) -> p g i", i=P)
            q = stage[:, 1, 0:H].rearrange("p (g i) -> p g i", i=P)
            r = stage[:, 2, 0:H].rearrange("p (g i) -> p g i", i=P)

            def quantizer(t, done):
                steps = [done]

                def step(ins):
                    steps[0] += 1
                    ins.then_inc(quant_steps, 1)
                    if steps[0] < QSTEPS:
                        dve.wait_ge(quant_steps, t * QSTEPS + steps[0])
                return step, steps

            def group_scales(t):
                step, steps = quantizer(t, 0)
                dve.wait_ge(w_loaded, t * 16 + 16)
                nc.vector.tensor_reduce(top[:, :], w, AXX, ALU.max)
                step(nc.vector.tensor_reduce(low[:, :], w, AXX, ALU.min))
                step(nc.vector.scalar_tensor_tensor(out=absmax[:, :], in0=low[:, :], scalar=-1.0, in1=top[:, :],
                                                    op0=ALU.mult, op1=ALU.max))
                step(nc.vector.tensor_scalar(scale0[:, :], absmax[:, :], 1.0 / QMAX, None, ALU.mult))
                step(nc.vector.tensor_copy(half_hi[:, :], scale0[:, :]))
                step(nc.vector.tensor_tensor(half_lo[:, :], scale0[:, :], raw(half_hi[:, :]), ALU.subtract))
                step(nc.vector.scalar_tensor_tensor(out=rest[:, :], in0=raw(half_hi[:, :]), scalar=-QMAX, in1=absmax[:, :],
                                                    op0=ALU.mult, op1=ALU.add))
                step(nc.vector.scalar_tensor_tensor(out=rest[:, :], in0=half_lo[:, :], scalar=-QMAX, in1=rest[:, :],
                                                    op0=ALU.mult, op1=ALU.add))
                step(nc.vector.scalar_tensor_tensor(out=scale[:, :], in0=rest[:, :], scalar=1.0 / QMAX, in1=scale0[:, :],
                                                    op0=ALU.mult, op1=ALU.add))
                step(nc.vector.tensor_scalar(isz[:, :], scale[:, :], 0.0, None, ALU.is_le))
                step(nc.vector.tensor_tensor(safe[:, :], scale[:, :], isz[:, :], ALU.add))
                nc.vector.reciprocal(inv[:, :], safe[:, :])
                step(nc.vector.tensor_copy(half_hi[:, :], safe[:, :]))
                step(nc.vector.tensor_tensor(half_lo[:, :], safe[:, :], raw(half_hi[:, :]), ALU.subtract))
                assert steps[0] == SCALE_STEPS

            def quotients(t, n, begin):
                half_steps = QUOT_STEPS // 2
                step, steps = quantizer(t, SCALE_STEPS + n * QUOT_STEPS + (0 if begin else half_steps))
                g = slice(n * KT // 2, (n + 1) * KT // 2)
                bc = lambda a: a[:, g, None].to_broadcast([P, KT // 2, P])
                tt = nc.vector.tensor_tensor

                def take_product(a, b):
                    step(tt(part[:, :, :], a, bc(b), ALU.mult))
                    step(tt(r[:, g, :], r[:, g, :], part[:, :, :], ALU.subtract))

                if begin:
                    if n == 0:
                        dve.wait_ge(tr_done, t * TR + KT)
                    step(tt(q[:, g, :], w[:, g, :], bc(inv), ALU.mult))
                    step(nc.vector.tensor_copy(quot_hi[:, :, :], q[:, g, :]))
                    tt(quot_lo[:, :, :], q[:, g, :], raw(quot_hi[:, :, :]), ALU.subtract)
                    step(tt(part[:, :, :], raw(quot_hi[:, :, :]), bc(raw(half_hi[:, :])), ALU.mult))
                    step(tt(r[:, g, :], w[:, g, :], part[:, :, :], ALU.subtract))
                    take_product(raw(quot_hi[:, :, :]), half_lo)
                    assert steps[0] == SCALE_STEPS + n * QUOT_STEPS + half_steps
                    return
                take_product(quot_lo[:, :, :], raw(half_hi[:, :]))
                take_product(quot_lo[:, :, :], half_lo)
                step(tt(r[:, g, :], r[:, g, :], bc(inv), ALU.mult))
                step(tt(q[:, g, :], q[:, g, :], r[:, g, :], ALU.add))
                assert steps[0] == SCALE_STEPS + (n + 1) * QUOT_STEPS

            def fake_quantized(t):
                step, steps = quantizer(t, SCALE_STEPS + 2 * QUOT_STEPS)
                bc = scale[:, :, None].to_broadcast([P, KT, P])
                step(nc.vector.tensor_scalar(q, q, ROUND, ROUND, ALU.add, ALU.subtract))
                step(nc.vector.tensor_scalar(q, q, QMAX, QMIN, ALU.min, ALU.max))
                step(nc.vector.tensor_tensor(q, q, bc, ALU.mult))
                step(nc.vector.tensor_tensor(q, q, w, ALU.subtract))
                step(nc.vector.tensor_tensor(r, w, q, ALU.add))
                assert steps[0] == QSTEPS

            def body(t, u, i):
                last = isinstance(t, int) and t == NCH - 1
                dve.wait_ge(wo_hi_done, t + 1)
                dve.wait_ge(wo_stored, t * 32 + CREDIT)
                nc.vector.tensor_tensor(wo_lo[:, :], stage[:, WO_STAGE, 0:H], raw(wo_hi[:, :]),
                                        ALU.subtract).then_inc(wo_lo_done, 1)
                for c in range(MM):
                    dve.wait_ge(mm_hi, t * MM + c + 1)
                    bank = mm_ps[mm_ring.bank[c]]
                    if c == 0:
                        dve.wait_ge(kv_stored, t * 64 + CREDIT)
                        nc.vector.tensor_tensor(k_lo[:, :], bank[0:D, :], raw(k_hi[:, :]), ALU.subtract).then_inc(mm_free, 1)
                    else:
                        dve.wait_ge(q_stored[(c - 1) % 2], t * (32 * QC // 2) + 32 * ((c - 1) // 2) + CREDIT)
                        nc.vector.scalar_tensor_tensor(out=q_lo[:, (c - 1) % 2, :], in0=bank[:, :], scalar=qscale[:, c - 1:c],
                                                       in1=raw(q_hi[:, (c - 1) % 2, :]),
                                                       op0=ALU.mult, op1=ALU.subtract).then_inc(mm_free, 1)
                    if c == 1:
                        dve.wait_ge(tr_done, tr_uses(t, TR_V))
                        nc.vector.tensor_copy(v_sb[:, :, :], tr_ps[tr_ring.bank[TR_V]][:, 0:SUB * D]
                                              .rearrange("p (s d) -> p s d", d=D)).then_inc(tr_free, 1)
                    if 3 <= c <= 6 and not last:
                        for k in (2 * (c - 3), 2 * (c - 3) + 1):
                            dve.wait_ge(tr_hi, t * (KT + 2) + (KT + k + 1))
                            nc.vector.tensor_tensor(xt_lo[:, 1 - u, k, :], tr_ps[tr_ring.bank[TR_X + k]][:, :],
                                                    raw(xt_hi[:, 1 - u, k, :]), ALU.subtract).then_inc(tr_free, 1)
                    if c == 0:
                        group_scales(t)
                    if c <= 3:
                        quotients(t, c // 2, c % 2 == 0)
                    elif c == 4:
                        fake_quantized(t)
                    if c == 7:
                        dve.wait_ge(wf_stored, t * 32 + CREDIT)
                        for h in range(2):
                            dve.wait_ge(tr_hi, t * (KT + 2) + (KT + h + 1 + (0 if last else KT)))
                            nc.vector.tensor_tensor(wf_lo[:, h * 4:h * 4 + 4, :],
                                                    tr_ps[tr_ring.bank[TR_W + h]][:, :].rearrange("p (j o) -> p j o", o=P),
                                                    raw(wf_hi[:, h * 4:h * 4 + 4, :]), ALU.subtract).then_inc(tr_free, 1)

            run_loop(dve, NCH, 2, body)


def attend(nc, distance_h, qrows_h, krows_h, ident_h, slope_h, q_hi_d, q_lo_d, k_d, v_d, att_d, sums_d, recip_d,
           wo_d, wf_d, w3, w3_in):
    ITS = B * NG
    QB = S // P
    HALF = S // CH
    BPH = CH // P
    KR = 3 * D + 4 + SPANS
    SLOTS = 3

    pieces = [(0, h, qb, 0, (qb + 1) * P) for h in range(HPG) for qb in range(BPH)]
    pieces += [(1, h, qb, k0, min((qb + 1) * P - k0, CH)) for h in range(HPG) for qb in range(BPH, QB) for k0 in (0, CH)]
    units = [(c, i) for c in range(HALF) for i in range(BPH * (c + 1))]

    def span(unit):
        c, i = unit
        lo = max(CH * c, P * i)
        return lo, CH * (c + 1) - lo

    def heads_at_once(unit):
        return {CH: 1, 3 * P: 1, 2 * P: 2, P: 4}[span(unit)[1]]

    scores_of, n = [], 0
    for unit in units:
        scores_of.append(n)
        n += HPG // heads_at_once(unit)
    SC = n
    NU = len(units)
    share = [4, 5, 4, 3, 4, 5, 5, 5, 5, 4, 3, 1]
    assert sum(share) == len(pieces)
    T_AT = {5: 0, 11: 1}
    MX = len(pieces) + len(T_AT)
    EXPS = HPG * NU
    exps_through = []
    for n, unit in enumerate(units):
        exps_through += [HPG * n + heads_at_once(unit) * (j + 1) for j in range(HPG // heads_at_once(unit))]
    order, at = [], 0
    for n in range(NU):
        order.append([("piece", at + j) for j in range(share[n])] + ([("turn", T_AT[n])] if n in T_AT else []))
        at += share[n]
    flat = [x for o in order for x in o]
    mx_use = {x: n for n, x in enumerate(flat)}
    mx_ring, sc_ring = Ring(MX, 2), Ring(SC, 4)
    PR = 3
    PUTS = 16 * 2 * HPG
    DIAG = [n for n, (c, i) in enumerate(units) if i >= BPH * c]

    ctx = ExitStack()
    with ctx:
        def sb(name, shape, dt=fp32):
            return ctx.enter_context(nc.sbuf_tensor(name, shape, dt))

        def sem(name):
            return ctx.enter_context(nc.semaphore(name))

        q3 = [sb(f"q3_{n}", [P, HPG, S], f32r) for n in range(SLOTS)]
        k3 = [sb(f"k3_{n}", [P, S], f32r) for n in range(SLOTS)]
        v = [sb(f"v_{n}", [P, QB, D]) for n in range(SLOTS)]
        probs = sb("probs", [P, PR, HPG, CH])
        distance = sb("distance", [P, S])
        ident = sb("ident2", [P, P])
        slope = sb("slope", [P, NH])
        ones = sb("ones", [P, D])
        credit = sb("credit2", [P, 6])
        unused = sb("unused", [P, 2, CH], bf16)
        mx = sb("mx", [P, 3 * BPH * HPG])
        mx1 = sb("mx1", [P, BPH * HPG])
        mxt_hi, mxt_lo = sb("mxt_hi", [BPH * HPG, HALF, P], f32r), sb("mxt_lo", [BPH * HPG, HALF, P], f32r)
        att, sums = sb("att", [P, HALF, CH]), sb("sums", [P, HALF, CH])
        EARLY = ITS - 4
        early, late = sb("early", [EARLY * HPG, S]), sb("late", [P, P])
        psum = [ctx.enter_context(nc.psum_tensor(f"pa{n}", [P, CH], fp32)) for n in range(8)]
        sc_ps, mx_ps, out_ps, sum_ps = psum[:4], psum[4:6], psum[6], psum[7]

        consts_in, rows_set, ones_set = sem("consts_in2"), sem("rows_set"), sem("ones_set")
        loaded = [sem(f"loaded{n}") for n in range(SLOTS)]
        neg_max = [[sem(f"neg_max{n}{c}") for c in range(HALF)] for n in range(SLOTS)]
        sc_done = sem("sc_done")
        mx_done, mx_free = sem("mx_done"), sem("mx_free")
        mx1_done = sem("mx1_done")
        mxt_hi_done = sem("mxt_hi_done")
        exp_done, cut_done = sem("exp_done"), sem("cut_done")
        pv_done, att_done = sem("pv_done"), sem("att_done")
        sums_back, recip_done, recip_stored = sem("sums_back"), sem("recip_done"), sem("recip_stored")
        att_stored = [sem(f"att_stored{c}") for c in range(HALF)]
        block = ctx.enter_context(nc.Block())

        def piece_cols(p):
            return p if p < 16 else 16 + (p - 16) // 2 + 16 * ((p - 16) % 2)

        def load(sp, t, u):
            b, g = t // NG, t % NG
            tok = bass.ds(b * S, S)
            for row, half in ((0, q_hi_d), (D, q_hi_d), (2 * D, q_lo_d)):
                src = half[bass.ds(g, 1), :, tok].rearrange("g (h d) q -> d (g h) q", d=D)
                sp.dma_start(raw(q3[u][row:row + D, :, :]), src).then_inc(loaded[u], 16)
            sp.dma_start(raw(k3[u][0:3 * D, :]), k_d[:, tok]).then_inc(loaded[u], 16)
            sp.dma_start(v[u][:, :, :], v_d[:, bass.ds(b * QB, QB), :]).then_inc(loaded[u], 16)

        def put_max(sp, t, u, c):
            sp.wait_ge(mx_free, MX * t + MX + mx_use[("turn", c)] + 1)
            for row, half in ((3 * D + 2, mxt_hi), (3 * D + 3, mxt_lo)):
                for h in range(HPG):
                    sp.dma_start(raw(q3[u][row:row + 1, h, c * CH:(c + 1) * CH]), raw(half[h * BPH:(h + 1) * BPH, c, :])).then_inc(neg_max[u][c], 16)

        def put_att(sp, t, c):
            b, g = t // NG, t % NG
            sp.wait_ge(att_done, t * HALF + (c + 1) + CREDIT)
            sp.dma_start(att_d[bass.ds(g, 1), :, bass.ds(b * S + c * CH, CH)].rearrange("g p q -> p (g q)"), att[:, c, :]).then_inc(att_stored[c], 16)
            sp.dma_start(sums_d[bass.ds(t, 1), :, c * CH:(c + 1) * CH].rearrange("t h q -> (t h) q"),
                         sums[0:P:D, c, :]).then_inc(att_stored[c], 16)

        early_d = [d[0:EARLY].rearrange("t h q -> (t h) q") for d in (sums_d, recip_d)]
        late_d = [d[EARLY:ITS].rearrange("t h (a q) -> (t h a) q", q=P) for d in (sums_d, recip_d)]

        @block.sync
        def _(sp):
            q_rows_in = probs[3 * D:KR, 0:2, :, :].rearrange("r a b q -> r (a b q)").rearrange("r (h q) -> r h q", h=HPG)
            load(sp, 0, 0)
            sp.dma_start(distance[:, :], distance_h).then_inc(consts_in, 16)
            sp.dma_start(ident[:, :], ident_h).then_inc(consts_in, 16)
            sp.dma_start(q_rows_in, qrows_h[:, None, :].to_broadcast([KR - 3 * D, HPG, S])).then_inc(consts_in, 16)
            sp.dma_start(probs[3 * D:KR, 2, 0:2, :], krows_h.rearrange("r (a q) -> r a q", a=2)).then_inc(consts_in, 16)
            sp.dma_start(slope[:, :], slope_h).then_inc(consts_in, 16)
            load(sp, 1, 1)
            sp.wait_ge(rows_set, 2 * SLOTS)
            put_max(sp, 0, 0, 0)
            put_max(sp, 0, 0, 1)

            def body(t, u, i):
                first, last, before_last = (isinstance(t, int) and t == n for n in (0, ITS - 1, ITS - 2))
                if not first:
                    put_att(sp, t - 1, 1)
                if not last and not before_last:
                    if not first:
                        sp.wait_ge(pv_done, t * NU + PR)
                    load(sp, t + 2, (u + 2) % SLOTS)
                if first:
                    for w, src, arrived in zip(w3, (wo_d[0], wo_d[1], wf_d[0]), w3_in):
                        sp.dma_start(raw(w[:, :, :]), src).then_inc(arrived, 16)
                if last:
                    for c in range(HALF):
                        sp.wait_ge(att_stored[c], EARLY * 32 + CREDIT)
                    sp.dma_start(early[:, :], early_d[0]).then_inc(sums_back, 16)
                put_att(sp, t, 0)
                if not last:
                    put_max(sp, t + 1, (u + 1) % SLOTS, 0)
                    put_max(sp, t + 1, (u + 1) % SLOTS, 1)

            slot_loop(sp, ITS, SLOTS, body)
            put_att(sp, ITS - 1, 1)
            for c in range(HALF):
                sp.wait_ge(att_stored[c], 32 * ITS + CREDIT)
            sp.dma_start(late[:, :], late_d[0]).then_inc(sums_back, 16)
            sp.wait_ge(recip_done, 1)
            sp.dma_start(early_d[1], early[:, :]).then_inc(recip_stored, 16)
            sp.wait_ge(recip_done, 2)
            sp.dma_start(late_d[1], late[:, :]).then_inc(recip_stored, 16)
            sp.wait_ge(recip_stored, 32)

        @block.gpsimd
        def _(pool):
            for n, (count, first) in enumerate(((mx_free, MX), (exp_done, EXPS), (pv_done, PR), (att_done, CREDIT),
                                                (att_stored[0], CREDIT), (att_stored[1], CREDIT))):
                pool.memset(credit[:, n:n + 1], 0.0).then_inc(count, first)
            pool.memset(ones[:, :], 1.0).then_inc(ones_set, 1)
            exps = Tally(pool, "exps", 2 * EXPS + HPG * (DIAG[0] + 1))

            def body(t, u, i):
                for d, n in enumerate(DIAG):
                    after = DIAG[d + 1] if d + 1 < len(DIAG) else NU + DIAG[0]
                    exps.wait(exp_done, t * EXPS + (EXPS + HPG * (n + 1)), HPG * (after - n))
                    block_of = probs[:, n % PR, :, 0:P]
                    nc.gpsimd.affine_select(out=block_of, in_=block_of, compare_op=ALU.is_ge, fill=0.0, base=0,
                                            pattern=[[0, HPG], [1, P]], channel_multiplier=-1).then_inc(cut_done, 1)

            slot_loop(pool, ITS, SLOTS, body)

        @block.tensor
        def _(pe):
            def maxima_item(w, u, item):
                kind, m = item
                n = mx_use[item]
                pe.wait_ge(mx_free, mx_ring.free(w, n))
                bank = mx_ps[mx_ring.bank[n]]
                if kind == "piece":
                    _, h, qb, k0, keys = pieces[m]
                    nc.tensor.matmul(bank[:, 0:keys], q3[u][0:3 * D, h, qb * P:(qb + 1) * P], k3[u][0:3 * D, k0:k0 + keys],
                                     start=True, stop=True).then_inc(mx_done, 1)
                    return
                if m == 0:
                    pe.wait_ge(mx_free, w * MX + (MX + mx_use[("piece", 4 * HPG - 1)] + 1))
                    src = mx[:, 0:BPH * HPG]
                else:
                    pe.wait_ge(mx1_done, w + 1)
                    src = mx1[:, :]
                nc.tensor.transpose(bank[0:BPH * HPG, 0:P], src, ident[:, :]).then_inc(mx_done, 1)

            def scores(t, u, n, j):
                _, kb = units[n]
                lo, N = span(units[n])
                heads = heads_at_once(units[n])
                use = scores_of[n] + j
                p = sc_ring.prev[use]
                before = exps_through[p] if p >= 0 else exps_through[p + SC] - EXPS
                pe.wait_ge(exp_done, t * EXPS + (EXPS + before))
                bank = sc_ps[sc_ring.bank[use]][:, 0:heads * N].rearrange("p (h q) -> p h q", h=heads)
                nc.tensor.matmul(bank, k3[u][0:KR, kb * P:(kb + 1) * P], q3[u][0:KR, j * heads:(j + 1) * heads, lo:lo + N],
                                 start=True, stop=True).then_inc(sc_done, 1)

            def values(t, u, n, part, pair):
                c, kb = units[n]
                lo, N = span(units[n])
                if part == 0 and pair == 0:
                    if n in DIAG:
                        pe.wait_ge(cut_done, t * len(DIAG) + DIAG.index(n) + 1)
                    else:
                        pe.wait_ge(exp_done, t * EXPS + (EXPS + HPG * (n + 1)))
                    if kb == 0:
                        pe.wait_ge(att_done, t * HALF + c + CREDIT)
                o, w = ((out_ps, v[u][:, kb, :]), (sum_ps, ones[:, :]))[part]
                for h in (2 * pair, 2 * pair + 1):
                    last = nc.tensor.matmul(o[h * D:(h + 1) * D, lo - c * CH:lo - c * CH + N], w, probs[:, n % PR, h, 0:N],
                                            start=(kb == 0), stop=(kb == BPH * (c + 1) - 1))
                if part == 1 and pair == 1:
                    last.then_inc(pv_done, 1)

            pe.wait_ge(consts_in, 16 * 5)
            pe.wait_ge(loaded[0], 80)
            for item in flat:
                maxima_item(0, 0, item)
            pe.wait_ge(rows_set, 2 * SLOTS)
            pe.wait_ge(ones_set, 1)

            def body(t, u, i):
                first, last = isinstance(t, int) and t == 0, isinstance(t, int) and t == ITS - 1
                nu = (u + 1) % SLOTS
                if not last:
                    pe.wait_ge(loaded[nu], (i + (2 if nu == 0 else 1)) * 80)
                for n in range(NU):
                    items = [] if last else list(order[n])
                    turn = items.pop() if items and n == NU - 1 else None
                    total = len(items)

                    def maxima_up_to(share_done):
                        while items and total - len(items) < share_done * total:
                            maxima_item(t + 1, nu, items.pop(0))

                    maxima_up_to(1 / 6)
                    if n in (0, BPH):
                        pe.wait_ge(neg_max[u][n // BPH], (i + 1) * PUTS)
                    uses = HPG // heads_at_once(units[n])
                    for j in range(uses):
                        scores(t, u, n, j)
                        if j == uses // 2 - 1:
                            maxima_up_to(2 / 6)
                    maxima_up_to(3 / 6)
                    if n or not first:
                        prev = (t, u, n - 1) if n else (t - 1, (u + 2) % SLOTS, NU - 1)
                        for part in range(2):
                            for pair in range(2):
                                values(*prev, part, pair)
                                maxima_up_to((4 + 2 * part + pair) / 6)
                    maxima_up_to(1)
                    if turn:
                        maxima_item(t + 1, nu, turn)

            slot_loop(pe, ITS, SLOTS, body)
            for part in range(2):
                for pair in range(2):
                    values(ITS - 1, (ITS - 1) % SLOTS, NU - 1, part, pair)

        @block.scalar
        def _(act):
            act.wait_ge(consts_in, 16 * 5)
            for n in range(SLOTS):
                nc.scalar.copy(q3[n][3 * D:KR, :, :].rearrange("r h q -> r (h q)"),
                               probs[3 * D:KR, 0:2, :, :].rearrange("r a b q -> r (a b q)")).then_inc(rows_set, 1)
                nc.scalar.copy(k3[n][3 * D:KR, :].rearrange("r (a q) -> r a q", a=2),
                               probs[3 * D:KR, 2, 0:2, :]).then_inc(rows_set, 1)
            act.wait_ge(rows_set, 2 * SLOTS)
            scored = Tally(act, "scored", SC + 1)

            def body(t, u, i):
                g = t % NG
                for n in range(NU):
                    _, N = span(units[n])
                    heads = heads_at_once(units[n])
                    act.wait_ge(pv_done, t * NU + (n + 1))
                    for h in range(HPG):
                        use = scores_of[n] + h // heads
                        if h % heads == 0:
                            scored.wait(sc_done, t * SC + (use + 1), 1)
                        at = (h % heads) * N
                        nc.scalar.activation(probs[:, n % PR, h, 0:N], sc_ps[sc_ring.bank[use]][:, at:at + N], ACT.Exp,
                                             scale=slope[:, bass.ds(g * HPG + h, 1)]).then_inc(exp_done, 1)

            slot_loop(act, ITS, SLOTS, body)

        @block.vector
        def _(dve):
            dve.wait_ge(consts_in, 16 * 5)
            items_done = Tally(dve, "items_done", 2 * MX + 1)

            def reduce_item(w, pu, pi, item):
                kind, m = item
                n = mx_use[item]
                items_done.wait(mx_done, w * MX + (n + 1), 1)
                bank = mx_ps[mx_ring.bank[n]]
                if kind == "piece":
                    _, h, qb, k0, keys = pieces[m]
                    d0 = S - P - qb * P + k0
                    col = piece_cols(m)
                    nc.vector.tensor_tensor_reduce(out=unused[:, mx_ring.bank[n], 0:keys], in0=bank[:, 0:keys], in1=distance[:, d0:d0 + keys],
                                                   scale=1.0, scalar=-3e38, op0=ALU.add, op1=ALU.max,
                                                   accum_out=mx[:, col:col + 1]).then_inc(mx_free, 1)
                    if m == len(pieces) - 1:
                        dve.wait_ge(mx_free, w * MX + (MX + n + 1))
                        k = BPH * HPG
                        nc.vector.tensor_tensor(mx1[:, :], mx[:, k:2 * k], mx[:, 2 * k:3 * k], ALU.max).then_inc(mx1_done, 1)
                    return
                if pu is not None:
                    dve.wait_ge(neg_max[pu][m], (pi + 1) * PUTS)
                src = bank[0:BPH * HPG, 0:P]
                nc.vector.tensor_scalar(mxt_hi[:, m, :], src, -1.0, None, ALU.mult).then_inc(mxt_hi_done, 1)
                dve.wait_ge(mxt_hi_done, w * HALF + (m + 1))
                nc.vector.scalar_tensor_tensor(out=mxt_lo[:, m, :], in0=src, scalar=-1.0, in1=raw(mxt_hi[:, m, :]),
                                               op0=ALU.mult, op1=ALU.subtract).then_inc(mx_free, 1)

            def evacuate(t, c):
                dve.wait_ge(pv_done, t * NU + (PR + BPH * (1 if c == 0 else 3)))
                dve.wait_ge(att_stored[c], t * 32 + CREDIT)
                nc.vector.tensor_copy(sums[:, c, :], sum_ps[:, :])
                nc.vector.tensor_copy(att[:, c, :], out_ps[:, :]).then_inc(att_done, 1)

            for item in flat:
                reduce_item(0, None, None, item)

            def body(t, u, i):
                first, last = isinstance(t, int) and t == 0, isinstance(t, int) and t == ITS - 1
                for n in range(NU):
                    items = [] if last else list(order[n])
                    turn = items.pop() if items and n == NU - 1 else None
                    for item in items:
                        reduce_item(t + 1, u, i, item)
                    if n == BPH:
                        evacuate(t, 0)
                    if n == 0 and not first:
                        evacuate(t - 1, 1)
                    if turn:
                        reduce_item(t + 1, u, i, turn)
                    if last and n == BPH:
                        dve.wait_ge(sums_back, 16)
                        nc.vector.reciprocal(early[:, :], early[:, :]).then_inc(recip_done, 1)

            slot_loop(dve, ITS, SLOTS, body)
            evacuate(ITS - 1, 1)
            dve.wait_ge(sums_back, 32)
            nc.vector.reciprocal(late[:, :], late[:, :]).then_inc(recip_done, 1)


def finish(nc, x, bias_h, ident_h, att_d, recip_d, wf_d, w3, w3_in, out):
    NT = T // P
    x_v = x.rearrange("b s h -> (b s) h").rearrange("(t p) h -> p t h", p=P)
    out_v = out.rearrange("b s h -> (b s) h").rearrange("(t p) h -> p t h", p=P)
    HV = H // CH
    LSTEPS = 8

    ctx = ExitStack()
    with ctx:
        def sb(name, shape, dt=fp32):
            return ctx.enter_context(nc.sbuf_tensor(name, shape, dt))

        def sem(name):
            return ctx.enter_context(nc.semaphore(name))

        wo_hi, wo_lo, wf_hi = w3
        wf_lo = sb("ff_lo", [P, KT, H], f32r)
        at_in = sb("at_in", [P, KT, P])
        recip = sb("recip", [P, KT, P])
        at_hi, at_lo = sb("at_hi", [P, 2, KT, P], f32r), sb("at_lo", [P, 2, KT, P], f32r)
        x_in = sb("x3_in", [P, 2, H])
        y = sb("y", [P, 2, H])
        yb = sb("yb", [P, H])
        yt_hi, yt_lo = sb("yt_hi", [P, KT, P], f32r), sb("yt_lo", [P, KT, P], f32r)
        z = sb("z", [P, 2, H])
        bias, credit = sb("bias", [P, H]), sb("credit3", [P, 2])
        ident = sb("ident3", [P, P])
        stats = [sb(f"stats{n}", [P, HV, 6]) for n in range(2)]
        mv = [sb(f"mv{n}", [P, 2]) for n in range(2)]
        var_eps, std, rstd0, ratio, fix, rstd = ([sb(f"ln{k}{n}", [P, 1]) for n in range(2)] for k in range(6))
        psum = [ctx.enter_context(nc.psum_tensor(f"pf{n}", [P, CH], fp32)) for n in range(6)]
        o_ps, f_ps, t_ps = psum[0:2], psum[2:4], psum[4:6]

        consts_in, wf_lo_in, at_norm = sem("consts_in3"), sem("wf_lo_in"), sem("at_norm")
        at_loaded, x_loaded = sem("at_loaded"), [sem(f"x3_loaded{n}") for n in range(2)]
        at_hi_done, at_lo_done = sem("at_hi_done"), sem("at_lo_done")
        o_done, y_sum, ln_steps = sem("o_done"), sem("y_sum"), [sem(f"ln_steps{n}") for n in range(2)]
        std_done = [sem(f"std_done{n}") for n in range(2)]
        yb_done, yt_turned, yt_hi_done, yt_lo_done = sem("yb_done"), sem("yt_turned"), sem("yt_hi_done"), sem("yt_lo_done")
        f_done, z_sum, stored = sem("f_done"), sem("z_sum"), [sem(f"stored{n}") for n in range(2)]
        block = ctx.enter_context(nc.Block())

        @block.sync
        def _(sp):
            sp.dma_start(bias[:, :], bias_h[None, :].to_broadcast([P, H])).then_inc(consts_in, 16)
            sp.dma_start(ident[:, :], ident_h).then_inc(consts_in, 16)
            def load(t, u):
                sp.dma_start(at_in[:, :, :], att_d[:, :, bass.ds(t * P, P)].rearrange("g p q -> p g q")).then_inc(at_loaded, 16)
                b, at = t // (S // P), (t % (S // P)) * P
                for h in range(HPG):
                    src = recip_d[bass.ds(b * NG, NG), h, bass.ds(at, P)]
                    sp.dma_start(recip[h * D:(h + 1) * D, :, :], src[None, :, :].to_broadcast([D, NG, P])).then_inc(at_loaded, 16)
                sp.dma_start(x_in[:, u:u + 1, :], x_v[:, bass.ds(t, 1), :]).then_inc(x_loaded[u], 16)
            load(0, 0)
            sp.dma_start(raw(wf_lo[:, :, :]), wf_d[1]).then_inc(wf_lo_in, 16)

            def body(t, u, i):
                first, last = isinstance(t, int) and t == 0, isinstance(t, int) and t == NT - 1
                if not last:
                    sp.wait_ge(at_lo_done, t + 1)
                    load(t + 1, 1 - u)
                if not first and not (isinstance(t, int) and t == 1):
                    store(t - 2, u)

            def store(t, u):
                sp.wait_ge(ln_steps[1], t * LSTEPS + LSTEPS)
                sp.dma_start(out_v[:, bass.ds(t, 1), :], z[:, u:u + 1, :]).then_inc(stored[u], 16)

            edge_loop(sp, NT, body)
            store(NT - 2, 0)
            store(NT - 1, 1)
            for u in range(2):
                sp.wait_ge(stored[u], NT // 2 * 16 + CREDIT)

        @block.tensor
        def _(pe):
            def product(ps, done, lhs, rhs, h):
                for k in range(KT):
                    for n, (a, w) in enumerate(((lhs[0], rhs[0]), (lhs[0], rhs[1]), (lhs[1], rhs[0]))):
                        last = nc.tensor.matmul(ps[h][:, :], a[:, k, :], w[:, k, h * CH:(h + 1) * CH],
                                                start=(k == 0 and n == 0), stop=(k == KT - 1 and n == 2))
                last.then_inc(done, 1)

            def linear(t, u):
                pe.wait_ge(yt_lo_done, t * 2 + 2)
                pe.wait_ge(z_sum, t * HV)
                if isinstance(t, int) and t == 0:
                    pe.wait_ge(w3_in[2], 16)
                    pe.wait_ge(wf_lo_in, 16)
                for h in range(HV):
                    product(f_ps, f_done, (yt_hi, yt_lo), (wf_hi, wf_lo), h)

            def turn(t, u):
                pe.wait_ge(ln_steps[0], t * LSTEPS + LSTEPS)
                pe.wait_ge(yt_lo_done, t * 2)
                for j in range(2):
                    for k in range(4):
                        cols = slice((j * 4 + k) * P, (j * 4 + k + 1) * P)
                        last = nc.tensor.transpose(t_ps[j][:, k * P:(k + 1) * P], y[:, u, cols], ident[:, :])
                    last.then_inc(yt_turned, 1)

            pe.wait_ge(consts_in, 32)
            pe.wait_ge(w3_in[0], 16)
            pe.wait_ge(w3_in[1], 16)

            def body(t, u, i):
                first = isinstance(t, int) and t == 0
                pe.wait_ge(at_lo_done, t + 1)
                pe.wait_ge(y_sum, t * HV)
                at = (at_hi[:, u, :, :], at_lo[:, u, :, :])
                product(o_ps, o_done, at, (wo_hi, wo_lo), 0)
                if not first:
                    turn(t - 1, 1 - u)
                product(o_ps, o_done, at, (wo_hi, wo_lo), 1)
                if not first:
                    linear(t - 1, 1 - u)

            edge_loop(pe, NT, body)
            turn(NT - 1, (NT - 1) % 2)
            linear(NT - 1, (NT - 1) % 2)

        @block.scalar
        def _(act):
            def split_hi(t, u, first=False):
                act.wait_ge(at_norm, t + 1)
                if not first:
                    act.wait_ge(o_done, (t - 1) * HV)
                nc.scalar.copy(at_hi[:, u, :, :], at_in[:, :, :]).then_inc(at_hi_done, 1)

            def root(t, which):
                act.wait_ge(ln_steps[which], t * LSTEPS + 3)
                nc.scalar.activation(std[which][:, :], var_eps[which][:, :], ACT.Sqrt).then_inc(std_done[which], 1)

            def turned_hi(t, first=False):
                if not first:
                    act.wait_ge(f_done, t * HV)
                for j in range(2):
                    act.wait_ge(yt_turned, t * 2 + (j + 1))
                    nc.scalar.copy(yt_hi[:, j * 4:j * 4 + 4, :], t_ps[j][:, :].rearrange("p (k q) -> p k q", q=P)).then_inc(yt_hi_done, 1)

            split_hi(0, 0, True)

            def body(t, u, i):
                first, second = (isinstance(t, int) and t == n for n in (0, 1))
                last = isinstance(t, int) and t == NT - 1
                if not first and not second:
                    root(t - 2, 1)
                if not first:
                    turned_hi(t - 1)
                if not last:
                    split_hi(t + 1, 1 - u, first)
                root(t, 0)

            edge_loop(act, NT, body)
            root(NT - 2, 1)
            turned_hi(NT - 1)
            root(NT - 1, 1)

        @block.gpsimd
        def _(pool):
            for u in range(2):
                pool.memset(credit[:, u:u + 1], 0.0).then_inc(stored[u], CREDIT)
            pool.wait_ge(consts_in, 32)

            def add_bias(t, u):
                pool.wait_ge(ln_steps[0], t * LSTEPS + LSTEPS)
                pool.wait_ge(z_sum, t * HV)
                nc.gpsimd.tensor_tensor(yb[:, :], y[:, u, :], bias[:, :], ALU.add).then_inc(yb_done, 1)

            def body(t, u, i):
                add_bias(t, u)

            edge_loop(pool, NT, body)

        @block.vector
        def _(dve):
            def normalize(t):
                dve.wait_ge(at_loaded, (t + 1) * 16 * (1 + HPG))
                nc.vector.tensor_tensor(at_in[:, :, :], at_in[:, :, :], recip[:, :, :], ALU.mult).then_inc(at_norm, 1)

            def split_lo(t, u):
                dve.wait_ge(at_hi_done, t + 1)
                nc.vector.tensor_tensor(at_lo[:, u, :, :], at_in[:, :, :], raw(at_hi[:, u, :, :]),
                                        ALU.subtract).then_inc(at_lo_done, 1)

            def sum_and_stats(t, u, which, h):
                done, ps, other, to, sums = ((o_done, o_ps, x_in[:, u, :], y, y_sum), (f_done, f_ps, yb, z, z_sum))[which]
                cols = slice(h * CH, (h + 1) * CH)
                dve.wait_ge(done, t * HV + (h + 1))
                nc.vector.tensor_tensor(to[:, u, cols], ps[h][:, :], other[:, cols], ALU.add).then_inc(sums, 1)
                dve.wait_ge(sums, t * HV + (h + 1))
                ins = nc.vector.bn_stats(stats[which][:, h, :], to[:, u, cols])
                if h == HV - 1:
                    ins.then_inc(ln_steps[which], 1)

            def norm(t, u, which):
                w, to = which, (y, z)[which]
                steps = [1]

                def step(ins):
                    steps[0] += 1
                    ins.then_inc(ln_steps[w], 1)
                    if steps[0] < LSTEPS:
                        dve.wait_ge(ln_steps[w], t * LSTEPS + steps[0])

                stats_done[w].wait(ln_steps[w], t * LSTEPS + 1, LSTEPS)
                step(nc.vector.bn_aggr(mv[w][:, :], stats[w][:, :, :]))
                step(nc.vector.tensor_scalar(var_eps[w][:, :], mv[w][:, 1:2], EPS, None, ALU.add))
                dve.wait_ge(std_done[w], t + 1)
                step(nc.vector.reciprocal(rstd0[w][:, :], std[w][:, :]))
                step(nc.vector.scalar_tensor_tensor(out=ratio[w][:, :], in0=rstd0[w][:, :], scalar=rstd0[w][:, :],
                                                    in1=var_eps[w][:, :], op0=ALU.mult, op1=ALU.mult))
                step(nc.vector.tensor_scalar(fix[w][:, :], ratio[w][:, :], -0.5, 1.5, ALU.mult, ALU.add))
                step(nc.vector.tensor_tensor(rstd[w][:, :], rstd0[w][:, :], fix[w][:, :], ALU.mult))
                step(nc.vector.tensor_scalar(to[:, u, :], to[:, u, :], mv[w][:, 0:1], rstd[w][:, :], ALU.subtract, ALU.mult))
                assert steps[0] == LSTEPS

            def turned_lo(t):
                if not (isinstance(t, int) and t == 0):
                    dve.wait_ge(f_done, t * HV)
                for j in range(2):
                    dve.wait_ge(yt_hi_done, t * 2 + (j + 1))
                    nc.vector.tensor_tensor(yt_lo[:, j * 4:j * 4 + 4, :], t_ps[j][:, :].rearrange("p (k q) -> p k q", q=P),
                                            raw(yt_hi[:, j * 4:j * 4 + 4, :]), ALU.subtract).then_inc(yt_lo_done, 1)

            def z_half(t, u, i, h):
                if h == 0:
                    dve.wait_ge(yb_done, t + 1)
                    dve.wait_ge(stored[u], i * 16 + CREDIT)
                sum_and_stats(t, u, 1, h)

            stats_done = [Tally(dve, f"stats_done{n}", first * LSTEPS + 1) for n, first in enumerate((2, 0))]
            normalize(0)
            split_lo(0, 0)

            def body(t, u, i):
                first, second = (isinstance(t, int) and t == n for n in (0, 1))
                last = isinstance(t, int) and t == NT - 1
                if not first and not second:
                    z_half(t - 2, u, i - 1, 1)
                    norm(t - 2, u, 1)
                    dve.wait_ge(yt_turned, (t - 1) * 2)
                    dve.wait_ge(yb_done, t - 1)
                dve.wait_ge(x_loaded[u], i * 16 + 16)
                sum_and_stats(t, u, 0, 0)
                if not last:
                    normalize(t + 1)
                if not first:
                    turned_lo(t - 1)
                sum_and_stats(t, u, 0, 1)
                norm(t, u, 0)
                if not last:
                    split_lo(t + 1, 1 - u)
                if not first:
                    z_half(t - 1, 1 - u, i if u == 1 else i - 1, 0)

            edge_loop(dve, NT, body)
            z_half(NT - 2, 0, NT // 2 - 1, 1)
            norm(NT - 2, 0, 1)
            turned_lo(NT - 1)
            z_half(NT - 1, 1, NT // 2 - 1, 0)
            z_half(NT - 1, 1, NT // 2 - 1, 1)
            norm(NT - 1, 1, 1)


_INS = ["L0_attn_hidden_states", "L0_attn_Wqkv", "L0_attn_Wo", "L0_ffn_weight", "L0_ffn_bias"]
_CONSTS = ["c_qscale", "c_distance", "c_qrows", "c_krows", "c_ident", "c_slope"]


def kernel(**inputs):
    import numpy as _np
    import concourse.bacc as _bacc
    from concourse import mybir as _mybir
    from concourse.bass_utils import run_bass_kernel_spmd as _run

    nc = _bacc.Bacc("TRN2", target_bir_lowering=False, num_devices=1)
    consts = shape_constants()
    arrays, args = {}, []
    for name in _INS + _CONSTS:
        a = _np.ascontiguousarray(inputs[name] if name in inputs else consts[name])
        arrays[f"in_{name}"] = a
        args.append(nc.dram_tensor(f"in_{name}", a.shape, _mybir.dt.from_np(a.dtype), kind="ExternalInput").ap())
    result = nc.dram_tensor("out_0", (B, S, H), _mybir.dt.float32, kind="ExternalOutput").ap()
    layer(nc, *args, result)
    r = _run(nc, [arrays], core_ids=[0])
    return r.results[0]["out_0"]
```
